# Optimizing a Trainium2 kernel written in Bass

```python
import numpy as np
import jax
import jax.numpy as jnp

def _softmax(x, axis=-1):
    return jax.nn.softmax(x, axis=axis)

def _gelu(x):
    return jax.nn.gelu(x, approximate=True)

def _silu(x):
    return jax.nn.silu(x)

def _sigmoid(x):
    return jax.nn.sigmoid(x)

def _layernorm(x, axis=-1, eps=1e-05):
    m = jnp.mean(x, axis=axis, keepdims=True)
    v = jnp.var(x, axis=axis, keepdims=True)
    return (x - m) / jnp.sqrt(v + eps)

def _scatter_add(tgt, idx, src, axis=0):
    return tgt.at[idx].add(src)

def _segment_sum(src, seg, n):
    return jax.ops.segment_sum(src, seg, n)
kernel_name = 'mk_gnn_ffn_d1_gnn_r32_e7085c'

def setup_inputs(seed: int=0):
    np.random.seed(seed)
    _w = jnp.asarray

    def _rec_inputs():
        import jax
        import jax.numpy as jnp
        _gk = jax.random.key(seed)
        x = -0.0002117 + 1 * jax.random.normal(jax.random.fold_in(_gk, 1), (3125, 256), jnp.float32)
        src = jax.random.randint(jax.random.fold_in(_gk, 2), (50000,), 0, 3125, jnp.int32)
        dst = jnp.minimum((3125 * jax.random.uniform(jax.random.fold_in(_gk, 3), (50000,)) ** 2.0).astype(jnp.int32), 99999)
        _o = jnp.argsort(dst, stable=True)
        src = src[_o]
        dst = dst[_o]
        edge_weight = jax.random.uniform(jax.random.fold_in(_gk, 12), (50000,), jnp.float32, 0.0, 0.999999)
        return (x, src, dst, edge_weight)
    x, src, dst, edge_weight = _rec_inputs()

    def _L0_gnn_setup():
        import jax, jax.numpy as jnp
        import numpy as np
        N = 3125
        E = 50000
        IN_FEATS = 256
        OUT_FEATS = 256
        EPS_WSUM = 1e-08
        EPS_NORM = 1e-12
        key = jax.random.key(seed)
        k1, k2, k3, k4, k5 = jax.random.split(key, 5)
        x = jax.random.normal(k1, (N, IN_FEATS), dtype=jnp.float32)
        edge_index = jax.random.randint(k2, (2, E), 0, N, dtype=jnp.int64)
        edge_weight = jax.random.uniform(k3, (E,), dtype=jnp.float32)
        lim = float(np.sqrt(6.0 / (IN_FEATS + OUT_FEATS)) * np.sqrt(2.0))
        W_self = jax.random.uniform(k4, (OUT_FEATS, IN_FEATS), dtype=jnp.float32, minval=-lim, maxval=lim)
        W_neigh = jax.random.uniform(k5, (OUT_FEATS, IN_FEATS), dtype=jnp.float32, minval=-lim, maxval=lim)
        bias = jnp.zeros((OUT_FEATS,), dtype=jnp.float32)
        return {'x': x, 'edge_index': edge_index, 'edge_weight': edge_weight, 'W_self': W_self, 'W_neigh': W_neigh, 'bias': bias}
    _L0_gnn_all = _L0_gnn_setup()
    _L0_gnn_in = {k: v for k, v in _L0_gnn_all.items() if k in ('W_self', 'W_neigh', 'bias')}
    del _L0_gnn_all

    def _L0_ffn_setup():
        import jax, jax.numpy as jnp
        import numpy as np
        C = 256
        EPS = 1e-05
        N_ITERS = 30

        def _layernorm(x, w, bias):
            mu = jnp.mean(x, axis=-1, keepdims=True)
            var = jnp.mean(jnp.square(x - mu), axis=-1, keepdims=True)
            return (x - mu) * jax.lax.rsqrt(var + EPS) * w + bias
        key = jax.random.key(seed)
        kx, kw, kb, klw, klb = jax.random.split(key, 5)
        x = jax.random.normal(kx, (8, 64, C), dtype=jnp.float32)
        bound = 1.0 / np.sqrt(C)
        W = jax.random.uniform(kw, (C, C), minval=-bound, maxval=bound, dtype=jnp.float32)
        b = jax.random.uniform(kb, (C,), minval=-bound, maxval=bound, dtype=jnp.float32)
        ln_w = jnp.ones((C,), dtype=jnp.float32)
        ln_b = jnp.zeros((C,), dtype=jnp.float32)
        return {'x': x, 'ln_w': ln_w, 'ln_b': ln_b, 'W': W, 'b': b}
    _L0_ffn_all = _L0_ffn_setup()
    _L0_ffn_in = {k: v for k, v in _L0_ffn_all.items() if k in ('ln_w', 'ln_b', 'W', 'b')}
    del _L0_ffn_all
    return {'x': x, 'src': src, 'dst': dst, 'edge_weight': edge_weight, 'L0_gnn_W_self': _L0_gnn_in['W_self'], 'L0_gnn_W_neigh': _L0_gnn_in['W_neigh'], 'L0_gnn_bias': _L0_gnn_in['bias'], 'L0_ffn_ln_w': _L0_ffn_in['ln_w'], 'L0_ffn_ln_b': _L0_ffn_in['ln_b'], 'L0_ffn_W': _L0_ffn_in['W'], 'L0_ffn_b': _L0_ffn_in['b']}

def reference(x, src, dst, edge_weight, L0_gnn_W_self, L0_gnn_W_neigh, L0_gnn_bias, L0_ffn_ln_w, L0_ffn_ln_b, L0_ffn_W, L0_ffn_b):
    import jax
    import jax.numpy as jnp

    def _L0_gnn_ref(x, edge_index, edge_weight, W_self, W_neigh, bias):
        import jax, jax.numpy as jnp
        import numpy as np
        N = 3125
        E = 50000
        IN_FEATS = 256
        OUT_FEATS = 256
        EPS_WSUM = 1e-08
        EPS_NORM = 1e-12
        row, col = (edge_index[0], edge_index[1])
        weighted = x[row] * edge_weight[:, None]
        num = jax.ops.segment_sum(weighted, col, num_segments=N)
        wsum = jax.ops.segment_sum(edge_weight, col, num_segments=N)
        wsum = jnp.maximum(wsum, EPS_WSUM)
        neigh = num / wsum[:, None]
        out = x @ W_self.T + neigh @ W_neigh.T + bias
        nrm = jnp.maximum(jnp.linalg.norm(out, axis=-1, keepdims=True), EPS_NORM)
        return out / nrm

    def _L0_ffn_ref(x, ln_w, ln_b, W, b):
        import jax, jax.numpy as jnp
        import numpy as np
        C = 256
        EPS = 1e-05
        N_ITERS = 30

        def _layernorm(x, w, bias):
            mu = jnp.mean(x, axis=-1, keepdims=True)
            var = jnp.mean(jnp.square(x - mu), axis=-1, keepdims=True)
            return (x - mu) * jax.lax.rsqrt(var + EPS) * w + bias

        def step(h, _):
            h = h + 0.01 * jnp.tanh(h)
            h = h * jax.nn.sigmoid(h)
            h = _layernorm(h, ln_w, ln_b)
            h = jnp.einsum('bsc,dc->bsd', h, W) + b
            return (h, None)
        x, _ = jax.lax.scan(step, x, None, length=N_ITERS)
        return x
    edge_index = jnp.stack([src, dst])
    x = x + _L0_gnn_ref(_layernorm(x, axis=-1), edge_index, edge_weight, L0_gnn_W_self, L0_gnn_W_neigh, L0_gnn_bias)
    x = x + _L0_ffn_ref(_layernorm(x, axis=-1)[None], L0_ffn_ln_w, L0_ffn_ln_b, L0_ffn_W, L0_ffn_b)[0]
    return x

_drawn_inputs = setup_inputs


def setup_inputs(seed=0):
    import zlib

    import numpy as np

    out = dict(_drawn_inputs(seed))
    spreads = {'L0_gnn_bias': (0.0, 0.732), 'L0_ffn_ln_w': (1.0, 0.2), 'L0_ffn_ln_b': (0.0, 0.1)}
    factors = {}
    for name, (base, spread) in spreads.items():
        noise = np.random.default_rng([zlib.crc32(name.encode()), seed]).standard_normal(out[name].shape)
        drawn = base * np.exp(spread * noise) if base else spread * noise
        out[name] = jnp.asarray(drawn.astype(out[name].dtype))
    for name, factor in factors.items():
        out[name] = (out[name] * factor).astype(out[name].dtype)
    return out
```

```python
from contextlib import ExitStack

import concourse.bass as bass
from concourse import mybir

F32 = mybir.dt.float32
I32 = mybir.dt.int32
ALU = mybir.AluOpType
ACT = mybir.ActivationFunctionType
AX_X = mybir.AxisListType.X


def gnn_ffn_kernel(nc, x, src, dst, edge_weight, w_self, w_neigh, gnn_bias, ln_w, ln_b, w_ffn, b_ffn, out):
    N, C = x.shape
    E = src.shape[0]
    STEPS = 30
    LN_EPS = 1e-5
    EPS_WSUM = 1e-8
    EPS_NORM = 1e-12
    P = 125
    NT = N // P
    KC = C // 128
    GT = 5
    NG = NT // GT
    W = 64
    W_SHIFT = 6
    EG = 256
    RQ = 98
    GROUPS = 2 * RQ
    LAST = E - (GROUPS - 1) * EG
    SPAN = N + W
    RING = 8
    HALF = RING // 2
    BODIES = GROUPS * 2 // RING
    assert N == NT * P and NT == NG * GT and C == 256 and 0 < LAST <= EG and E >= EG
    assert GROUPS * 2 % RING == 0 and 1 << W_SHIFT == W

    ln1_dram = nc.dram_tensor("ln1_scratch", [N, C], F32, kind="Internal").ap()

    with ExitStack() as ctx:
        def sb(name, shape, dt=F32):
            return ctx.enter_context(nc.sbuf_tensor(name, shape, dt))

        def sem(name):
            return ctx.enter_context(nc.semaphore(name))

        x_sb = sb("x_sb", [P, NT, C])
        y_sb = sb("y_sb", [P, NT, C])
        work = sb("work", [P, NT, C])
        hT = sb("hT", [128, NT, KC, P])
        numT = sb("numT", [128, KC + 1, SPAN])
        iota_f = sb("iota_f", [128, SPAN])
        small_i = sb("small_i", [128, 2, EG], I32)
        rows_w = sb("rows_w", [128, 2, EG])
        rows_d = sb("rows_d", [128, 2, EG])
        rows_s = sb("rows_s", [128, 2, EG])
        src_i = sb("src_i", [128, 2, EG], I32)
        tab_cols = sb("tab_cols", [128, 4])
        tab_max = sb("tab_max", [128, 2])
        tab_int = sb("tab_int", [128, 2], I32)
        tab = sb("tab", [1, 2, GROUPS], I32)
        dstT = sb("dstT", [128, GROUPS, 2])
        wT = sb("wT", [128, GROUPS, 2])
        srcT = sb("srcT", [128, GROUPS * 2 + RING], I32)
        idx = sb("idx", [128, RING], I32)
        gath = sb("gath", [128, RING, C])
        onehot = sb("onehot", [128, 2, W])
        ident = sb("ident", [128, 128])
        ones = sb("ones", [128, 128])
        w_raw = sb("w_raw", [128, 3, KC, C])
        w_fold = sb("w_fold", [128, KC, C])
        wT_all = sb("wT_all", [128, 4, KC, C])
        rowmean = sb("rowmean", [128, KC])
        lnw_bc = sb("lnw_bc", [128, C])
        bias_bc = sb("bias_bc", [P, C])
        bff_bc = sb("bff_bc", [P, C])
        lnb_col = sb("lnb_col", [128, KC])
        lnb_mat = sb("lnb_mat", [128, KC, P])
        st = sb("st", [P, NT, 6])
        mv = sb("mv", [P, NT, 2])
        rstd = sb("rstd", [P, NT])
        ssq = sb("ssq", [P, NT])
        sd = sb("sd", [P, NT])
        mhalf = sb("mhalf", [P, GT])
        quarter = sb("quarter", [P, GT])
        ceps = sb("ceps", [P, GT])
        pl = sb("pl", [P, NG, 6, GT])

        psA = ctx.enter_context(nc.psum_tensor("psA", [128, 2, 512], F32))
        psB = ctx.enter_context(nc.psum_tensor("psB", [128, 2, 1536], F32))

        s_dst = sem("dst_loaded")
        s_src = sem("src_loaded")
        s_wts = sem("edge_weights_loaded")
        s_x = sem("x_loaded")
        s_par = sem("parameters_loaded")
        s_ident = sem("ident_made")
        s_cst = sem("constants_made")
        s_dve = sem("vector_chain")
        s_act = sem("scalar_chain")
        s_tabT = sem("table_transposed")
        s_tabE = sem("table_evicted")
        s_stat0 = sem("x_stats_ready")
        s_ln1 = sem("ln1_made")
        s_ln1w = sem("ln1_in_dram")
        s_wTt = sem("weights_transposed")
        s_wTe = sem("weights_evicted")
        s_fold = sem("weights_folded")
        s_bff = sem("ffn_bias_product")
        s_xT = sem("ln1_transposed")
        s_xTe = sem("ln1T_evicted")
        s_self = sem("self_product")
        s_selfe = sem("self_evicted")
        s_idx = sem("indices_ready")
        s_g = [sem(f"gathered_{r}") for r in range(RING)]
        s_oh = sem("onehot_ready")
        s_go = sem("gathers_go")
        s_win = sem("window_product")
        s_num = sem("window_added")
        s_neigh = sem("neigh_ready")
        s_np = sem("neigh_product")
        s_gsum = sem("gnn_row_summed")
        s_ss = sem("row_squares_summed")
        s_sd = sem("deviation_ready")
        s_y = sem("rows_ready")
        s_tanh = sem("tanh_ready")
        s_u = sem("u_ready")
        s_silu = sem("silu_ready")
        s_bn = sem("stats_ready")
        s_rstd = sem("rstd_ready")
        s_pool = sem("pool_chain")
        s_hT = sem("h_transposed")
        s_hTe = sem("hT_evicted")
        s_z = sem("ffn_product")
        s_res = sem("result_ready")
        s_out = sem("out_written")

        block = ctx.enter_context(nc.Block())

        x_dram = x.rearrange("(t p) c -> p t c", p=P)
        ln1_out = ln1_dram.rearrange("(t p) c -> p t c", p=P)
        out_dram = out.rearrange("(t p) c -> p t c", p=P)
        PAIRS = [(0, 2), (2, 4), (4, 5)]

        def load_edges(eng, table, tile, s):
            full = table[0:RQ * EG].rearrange("(r k) -> r k", k=EG)
            eng.dma_start(tile[0:RQ, 0, :], full).then_inc(s, 16)
            rest = table[RQ * EG:(GROUPS - 1) * EG].rearrange("(r k) -> r k", k=EG)
            eng.dma_start(tile[0:RQ - 1, 1, :], rest).then_inc(s, 16)
            tail = table[(GROUPS - 1) * EG:E].rearrange("(a k) -> a k", a=1)
            eng.dma_start(tile[RQ - 1:RQ, 1, 0:LAST], tail).then_inc(s, 16)

        def fill_edges(eng, table, tile, s):
            fill = table[E - (EG - LAST):E].rearrange("(a k) -> a k", a=1)
            eng.dma_start(tile[RQ - 1:RQ, 1, LAST:EG], fill).then_inc(s, 16)

        @block.sync
        def _(sp):
            load_edges(sp, dst, small_i, s_dst)
            fill_edges(sp, dst, small_i, s_dst)
            sp.dma_start(x_sb[:], x_dram).then_inc(s_x, 16)
            for m, w in enumerate((w_self, w_neigh, w_ffn)):
                sp.dma_start(w_raw[:, m, :, :], w.rearrange("(k p) c -> p k c", p=128)).then_inc(s_par, 16)
            sp.dma_start(lnw_bc[:], ln_w.rearrange("(a c) -> a c", a=1).broadcast_to([128, C])).then_inc(s_par, 16)
            sp.dma_start(bias_bc[:], gnn_bias.rearrange("(a c) -> a c", a=1).broadcast_to([P, C])).then_inc(s_par, 16)
            sp.dma_start(bff_bc[:], b_ffn.rearrange("(a c) -> a c", a=1).broadcast_to([P, C])).then_inc(s_par, 16)
            sp.dma_start(lnb_col[:], ln_b.rearrange("(k p) -> p k", p=128), allow_slow_non_contiguous=True).then_inc(s_par, 16)
            sp.wait_ge(s_ln1, NT)
            sp.dma_start(ln1_out, work[:]).then_inc(s_ln1w, 16)
            for g in range(NG):
                sp.wait_ge(s_res, g + 1)
                sp.dma_start(out_dram[:, g * GT:(g + 1) * GT, :], y_sb[:, g * GT:(g + 1) * GT, :]).then_inc(s_out, 16)
            sp.wait_ge(s_out, 16 * NG)
            sp.wait_ge(s_ln1w, 16)

        @block.gpsimd
        def _(pool):
            nc.gpsimd.memset(ident[:], 0.0).then_inc(s_pool, 1)
            pool.wait_ge(s_pool, 1)
            nc.gpsimd.affine_select(out=ident[:], in_=ident[:], compare_op=ALU.not_equal, fill=1.0, base=0,
                                    pattern=[[-1, 128]], channel_multiplier=1).then_inc(s_ident, 1)
            nc.gpsimd.memset(ones[:], 1.0).then_inc(s_cst, 1)
            nc.gpsimd.iota(iota_f[:], pattern=[[1, SPAN]], base=0, channel_multiplier=0,
                           allow_small_or_imprecise_dtypes=True).then_inc(s_cst, 1)
            nc.gpsimd.memset(mhalf[:], -0.5).then_inc(s_cst, 1)
            nc.gpsimd.memset(quarter[:], C / 4.0).then_inc(s_cst, 1)
            nc.gpsimd.memset(ceps[:], C * LN_EPS).then_inc(s_cst, 1)
            pool.wait_ge(s_ln1w, 16)
            with pool.Fori(0, BODIES) as i:
                for half in range(2):
                    pool.wait_ge(s_idx, i * 2 + (half + 1))
                    pool.sem_inc(s_go, 1)
                    for r in range(half * HALF, (half + 1) * HALF):
                        nc.gpsimd.indirect_dma_start(
                            out=gath[:, r, :], out_offset=None, in_=ln1_dram[:, :],
                            in_offset=bass.IndirectOffsetOnAxis(ap=idx[:, r:r + 1], axis=0)).then_inc(s_g[r], 16)

            def rstd_of(k, g):
                sg = st[:, g * GT:(g + 1) * GT, :]
                pool.wait_ge(s_bn, (k + 1) * GT)
                nc.gpsimd.tensor_tensor(pl[:, g, 0, :], sg[:, :, 1], sg[:, :, 4], ALU.subtract).then_inc(s_pool, 1)
                nc.gpsimd.tensor_tensor(pl[:, g, 1, :], sg[:, :, 2], sg[:, :, 5], ALU.add).then_inc(s_pool, 1)
                pool.wait_ge(s_pool, k * 6 + 3)
                nc.gpsimd.tensor_tensor(pl[:, g, 2, :], pl[:, g, 0, :], pl[:, g, 0, :], ALU.mult).then_inc(s_pool, 1)
                pool.wait_ge(s_pool, k * 6 + 4)
                nc.gpsimd.tensor_tensor(pl[:, g, 3, :], pl[:, g, 2, :], quarter[:, :], ALU.mult).then_inc(s_pool, 1)
                pool.wait_ge(s_pool, k * 6 + 5)
                nc.gpsimd.tensor_tensor(pl[:, g, 4, :], pl[:, g, 3, :], pl[:, g, 1, :], ALU.add).then_inc(s_pool, 1)
                pool.wait_ge(s_pool, k * 6 + 6)
                nc.gpsimd.tensor_tensor(pl[:, g, 5, :], pl[:, g, 4, :], ceps[:, :], ALU.add).then_inc(s_pool, 1)
                pool.wait_ge(s_pool, k * 6 + 7)
                nc.gpsimd.tensor_tensor(rstd[:, g * GT:(g + 1) * GT], pl[:, g, 5, :], mhalf[:, :], ALU.pow).then_inc(s_rstd, 1)

            pool.wait_ge(s_cst, 5)
            pool.wait_ge(s_y, NG)
            with pool.Fori(0, STEPS) as it:
                for g in range(NG):
                    rstd_of(it * NG + g, g)

        @block.scalar
        def _(act):
            load_edges(act, src, src_i, s_src)
            fill_edges(act, src, src_i, s_src)
            act.wait_ge(s_dve, 1)
            load_edges(act, edge_weight, rows_w, s_wts)

            act.wait_ge(s_dve, 2)
            nc.scalar.activation(sd[:, :], rstd[:, :], ACT.Sqrt).then_inc(s_sd, 1)
            for m in range(4):
                act.wait_ge(s_wTt, m + 1)
                nc.scalar.copy(wT_all[:, m, :, :], psB[:, m % 2, 0:KC * C].rearrange("p (k c) -> p k c", k=KC)).then_inc(s_wTe, 1)
            for t in range(NT):
                act.wait_ge(s_xT, t + 1)
                nc.scalar.copy(hT[:, t, :, :], psA[:, t % 2, 0:KC * P].rearrange("p (k n) -> p k n", k=KC)).then_inc(s_xTe, 1)
            for t in range(NT):
                act.wait_ge(s_gsum, t + 1)
                nc.scalar.activation(work[:, t, :], y_sb[:, t, :], ACT.Square, accum_out=ssq[:, t:t + 1]).then_inc(s_ss, 1)
            act.wait_ge(s_ss, NT)
            nc.scalar.activation(sd[:, :], ssq[:, :], ACT.Sqrt).then_inc(s_sd, 1)
            act.wait_ge(s_dve, 6)
            nc.scalar.activation(sd[:, :], rstd[:, :], ACT.Sqrt).then_inc(s_sd, 1)

            def evict(k, g):
                for n, (a, b) in enumerate(PAIRS):
                    act.wait_ge(s_hT, k * 3 + (n + 1))
                    nc.scalar.copy(hT[:, g * GT + a:g * GT + b, :, :],
                                   psA[:, n % 2, 0:(b - a) * KC * P].rearrange("p (j k n) -> p j k n", k=KC, n=P)
                                   ).then_inc(s_hTe, 1)

            act.wait_ge(s_sd, 3)
            with act.Fori(0, STEPS) as it:
                for g in range(NG):
                    k = it * NG + g
                    rows = slice(g * GT, (g + 1) * GT)
                    act.wait_ge(s_y, k + 1)
                    nc.scalar.activation(work[:, rows, :], y_sb[:, rows, :], ACT.Tanh).then_inc(s_tanh, 1)
                    if g:
                        evict(k - 1, g - 1)
                    act.wait_ge(s_u, k + 1)
                    nc.scalar.activation(work[:, rows, :], work[:, rows, :], ACT.Silu).then_inc(s_silu, 1)
                evict(it * NG + (NG - 1), NG - 1)

        @block.vector
        def _(dve):
            nc.vector.memset(rows_w[:], 0.0).then_inc(s_dve, 1)
            nc.vector.memset(numT[:], 0.0).then_inc(s_num, 1)
            nc.vector.memset(srcT[:], 0).then_inc(s_tabE, 1)

            dve.wait_ge(s_x, 16)
            for t in range(NT):
                nc.vector.bn_stats(st[:, t, :], x_sb[:, t, :]).then_inc(s_stat0, 1)
            dve.wait_ge(s_stat0, NT)
            for t in range(NT):
                nc.vector.bn_aggr(mv[:, t, :], st[:, t, :]).then_inc(s_stat0, 1)
            dve.wait_ge(s_stat0, 2 * NT)
            nc.vector.tensor_scalar(rstd[:, :], mv[:, :, 1], LN_EPS, None, ALU.add).then_inc(s_dve, 1)
            dve.wait_ge(s_sd, 1)
            nc.vector.reciprocal(ssq[:, :], sd[:, :]).then_inc(s_dve, 1)
            dve.wait_ge(s_dve, 3)
            for t in range(NT):
                nc.vector.tensor_scalar(work[:, t, :], x_sb[:, t, :], mv[:, t, 0:1], ssq[:, t:t + 1],
                                        ALU.subtract, ALU.mult).then_inc(s_ln1, 1)

            dve.wait_ge(s_dst, 64)
            nc.vector.tensor_copy(rows_d[0:RQ, :, :], small_i[0:RQ, :, :]).then_inc(s_tabE, 1)
            dve.wait_ge(s_tabE, 2)
            nc.vector.tensor_reduce(tab_cols[0:RQ, 0:2], rows_d[0:RQ, :, :], AX_X, ALU.min).then_inc(s_tabE, 1)
            nc.vector.tensor_reduce(tab_max[0:RQ, :], rows_d[0:RQ, :, :], AX_X, ALU.max).then_inc(s_tabE, 1)
            dve.wait_ge(s_tabE, 4)
            nc.vector.tensor_tensor(tab_int[0:RQ, :], tab_max[0:RQ, :], tab_cols[0:RQ, 0:2], ALU.subtract).then_inc(s_tabE, 1)
            for q in range(2):
                nc.vector.tensor_scalar(rows_d[0:RQ, q, :], rows_d[0:RQ, q, :], tab_cols[0:RQ, q:q + 1], None,
                                        ALU.subtract).then_inc(s_tabE, 1)
            dve.wait_ge(s_tabE, 7)
            nc.vector.tensor_scalar(small_i[0:RQ, 0, 0:2], tab_int[0:RQ, :], W_SHIFT, None,
                                    ALU.arith_shift_right).then_inc(s_tabE, 1)
            dve.wait_ge(s_tabE, 8)
            nc.vector.tensor_scalar(tab_cols[0:RQ, 2:4], small_i[0:RQ, 0, 0:2], 1.0, None, ALU.add).then_inc(s_tabE, 1)
            dve.wait_ge(s_src, 64)
            nc.vector.tensor_copy(rows_s[0:RQ, :, :], src_i[0:RQ, :, :]).then_inc(s_tabE, 1)
            per = GROUPS * 2
            dve.wait_ge(s_tabT, 1)
            nc.vector.tensor_copy(srcT[:, 0:per].rearrange("p (g h) -> p h g", h=2),
                                  psA[:, 0, 0:per].rearrange("p (h g) -> p h g", h=2)).then_inc(s_tabE, 1)
            dve.wait_ge(s_tabT, 2)
            nc.vector.tensor_copy(dstT[:, :, :].rearrange("p g h -> p h g"),
                                  psA[:, 1, 0:per].rearrange("p (h g) -> p h g", h=2)).then_inc(s_tabE, 1)
            dve.wait_ge(s_tabT, 3)
            nc.vector.tensor_copy(tab[:, :, :], psB[0:1, 0, 0:2 * GROUPS].rearrange("p (a g) -> p a g", a=2)).then_inc(s_tabE, 1)
            dve.wait_ge(s_tabT, 4)
            nc.vector.tensor_copy(wT[:, :, :].rearrange("p g h -> p h g"),
                                  psB[:, 1, 0:per].rearrange("p (h g) -> p h g", h=2)).then_inc(s_tabE, 1)
            dve.wait_ge(s_tabE, 14)
            for half in range(2):
                a = half * HALF
                nc.vector.tensor_copy(idx[:, a:a + HALF], srcT[:, a:a + HALF]).then_inc(s_idx, 1)

            dve.wait_ge(s_par, 7 * 16)
            for k in range(KC):
                nc.vector.tensor_tensor(w_fold[:, k, :], w_raw[:, 2, k, :], lnw_bc[:, :], ALU.mult).then_inc(s_fold, 1)
            dve.wait_ge(s_fold, KC)
            nc.vector.tensor_reduce(rowmean[:, :], w_fold[:, :, :], AX_X, ALU.add).then_inc(s_fold, 1)
            dve.wait_ge(s_fold, KC + 1)
            nc.vector.tensor_scalar(tab_max[:, :], rowmean[:, :], 1.0 / C, None, ALU.mult).then_inc(s_fold, 1)
            dve.wait_ge(s_fold, KC + 2)
            for k in range(KC):
                nc.vector.tensor_scalar(w_fold[:, k, :], w_fold[:, k, :], tab_max[:, k:k + 1], float(C) ** 0.5,
                                        ALU.subtract, ALU.mult).then_inc(s_fold, 1)
            for k in range(KC):
                nc.vector.tensor_copy(lnb_mat[:, k, :], lnb_col[:, k:k + 1].broadcast_to([128, P])).then_inc(s_fold, 1)
            dve.wait_ge(s_bff, 1)
            nc.vector.tensor_tensor(bff_bc[:, :], bff_bc[:, :], psB[0:P, 0, 0:C], ALU.add).then_inc(s_fold, 1)
            for t in range(NT):
                dve.wait_ge(s_self, t + 1)
                nc.vector.tensor_tensor(y_sb[:, t, :], psB[0:P, (t + 1) % 2, 0:C], bias_bc[:, :], ALU.add).then_inc(s_selfe, 1)

            windows = dve.alloc_register("vector_windows")
            dve.reg_mov(windows, 0)
            column = dve.alloc_register("window_column")
            dve.wait_ge(s_num, 1)
            dve.wait_ge(s_cst, 5)
            with dve.Fori(0, BODIES) as i:
                for j in range(HALF):
                    g = i * HALF + j
                    base = dve.value_load(tab[0:1, 0, bass.ds(g, 1)], min_val=0, max_val=N - 1)
                    count = dve.value_load(tab[0:1, 1, bass.ds(g, 1)], min_val=1, max_val=SPAN // W)
                    done = dve.snap(windows, min_val=0, max_val=GROUPS * (SPAN // W))
                    dve.reg_mov(column, base)
                    with dve.Fori(0, count) as k:
                        for h in range(2):
                            nc.vector.tensor_scalar(onehot[:, h, :], iota_f[:, bass.ds(k * W, W)],
                                                    dstT[:, bass.ds(g, 1), h], wT[:, bass.ds(g, 1), h],
                                                    ALU.is_equal, ALU.mult).then_inc(s_oh, 1)
                        dve.wait_ge(s_win, done + k + 1)
                        at = dve.snap(column, min_val=0, max_val=N - 1)
                        cols = numT[:, :, bass.ds(at, W)]
                        nc.vector.tensor_tensor(cols, cols,
                                                psB[:, 0, 0:(KC + 1) * W].rearrange("p (c w) -> p c w", w=W),
                                                ALU.add).then_inc(s_num, 1)
                        dve.reg_add(column, column, W)
                    dve.reg_add(windows, windows, count)
                    if j % 2:
                        a = (j // 2) * HALF
                        nc.vector.tensor_copy(idx[:, a:a + HALF],
                                              srcT[:, bass.ds((i + 1) * RING + a, HALF)]).then_inc(s_idx, 1)

            dve.wait_ge(s_idx, 2 * BODIES + 2)
            nc.vector.tensor_scalar(numT[:, KC, 0:N], numT[:, KC, 0:N], EPS_WSUM, None, ALU.max).then_inc(s_neigh, 1)
            dve.wait_ge(s_neigh, 1)
            nc.vector.reciprocal(numT[:, KC, 0:N], numT[:, KC, 0:N]).then_inc(s_neigh, 1)
            dve.wait_ge(s_neigh, 2)
            for k in range(KC):
                nc.vector.tensor_tensor(numT[:, k, 0:N], numT[:, k, 0:N], numT[:, KC, 0:N], ALU.mult).then_inc(s_neigh, 1)
            for t in range(NT):
                dve.wait_ge(s_np, t + 1)
                nc.vector.tensor_tensor(y_sb[:, t, :], psB[0:P, t % 2, 0:C], y_sb[:, t, :], ALU.add).then_inc(s_gsum, 1)
            dve.wait_ge(s_sd, 2)
            nc.vector.tensor_scalar(rstd[:, :], sd[:, :], EPS_NORM, None, ALU.max).then_inc(s_dve, 1)
            dve.wait_ge(s_dve, 4)
            nc.vector.reciprocal(ssq[:, :], rstd[:, :]).then_inc(s_dve, 1)
            dve.wait_ge(s_dve, 5)
            for t in range(NT):
                nc.vector.scalar_tensor_tensor(out=x_sb[:, t, :], in0=y_sb[:, t, :], scalar=ssq[:, t:t + 1],
                                               in1=x_sb[:, t, :], op0=ALU.mult, op1=ALU.add).then_inc(s_neigh, 1)
            for t in range(NT):
                dve.wait_ge(s_neigh, 2 + KC + t + 1)
                nc.vector.bn_stats(st[:, t, :], x_sb[:, t, :]).then_inc(s_neigh, 1)
            dve.wait_ge(s_neigh, 2 + KC + 2 * NT)
            for t in range(NT):
                nc.vector.bn_aggr(mv[:, t, :], st[:, t, :]).then_inc(s_neigh, 1)
            dve.wait_ge(s_neigh, 2 + KC + 3 * NT)
            nc.vector.tensor_scalar(rstd[:, :], mv[:, :, 1], LN_EPS, None, ALU.add).then_inc(s_dve, 1)
            dve.wait_ge(s_sd, 3)
            nc.vector.reciprocal(ssq[:, :], sd[:, :]).then_inc(s_dve, 1)
            dve.wait_ge(s_dve, 7)
            for t in range(NT):
                ins = nc.vector.tensor_scalar(y_sb[:, t, :], x_sb[:, t, :], mv[:, t, 0:1], ssq[:, t:t + 1],
                                              ALU.subtract, ALU.mult)
                if t % GT == GT - 1:
                    ins.then_inc(s_y, 1)

            def rows_of(g):
                return slice(g * GT, (g + 1) * GT)

            def make_u(k, g):
                dve.wait_ge(s_tanh, k + 1)
                nc.vector.scalar_tensor_tensor(out=work[:, rows_of(g), :], in0=work[:, rows_of(g), :], scalar=0.01,
                                               in1=y_sb[:, rows_of(g), :], op0=ALU.mult, op1=ALU.add).then_inc(s_u, 1)

            def stats(k, g):
                dve.wait_ge(s_silu, k + 1)
                for t in range(g * GT, (g + 1) * GT):
                    nc.vector.bn_stats(st[:, t, :], work[:, t, :]).then_inc(s_bn, 1)

            def next_rows(k, g):
                dve.wait_ge(s_rstd, k + 1)
                for j in range(GT):
                    if j % 2 == 0:
                        dve.wait_ge(s_z, k * GT + min(j + 2, GT))
                    ins = nc.vector.scalar_tensor_tensor(
                        out=y_sb[:, g * GT + j, :], in0=psB[0:P, g % 2, j * C:(j + 1) * C],
                        scalar=rstd[:, g * GT + j:g * GT + j + 1], in1=bff_bc[:, :], op0=ALU.mult, op1=ALU.add)
                ins.then_inc(s_y, 1)

            def step(it, first):
                for g in range(NG):
                    k = it * NG + g
                    make_u(k, g)
                    if g < 2:
                        if not first:
                            next_rows(k - 2, g + NG - 2)
                    if g:
                        stats(k - 1, g - 1)
                    if g >= 2:
                        next_rows(k - 2, g - 2)
                stats(it * NG + NG - 1, NG - 1)

            step(0, True)
            with dve.Fori(1, STEPS) as it:
                step(it, False)
            for g in (NG - 2, NG - 1):
                next_rows((STEPS - 1) * NG + g, g)
            for g in range(NG):
                dve.wait_ge(s_y, (STEPS + 1) * NG - (NG - 1 - g))
                nc.vector.tensor_tensor(y_sb[:, rows_of(g), :], y_sb[:, rows_of(g), :], x_sb[:, rows_of(g), :],
                                        ALU.add).then_inc(s_res, 1)

        @block.tensor
        def _(pe):
            def transpose(o, i, n):
                return nc.tensor.transpose(o, i, ident[0:n, 0:n])

            pe.wait_ge(s_ident, 1)
            pe.wait_ge(s_tabE, 10)
            for table, o, s in ((rows_s, psA[:, 0, :], None), (rows_d, psA[:, 1, :], None)):
                for h in range(2):
                    for q in range(2):
                        at = h * GROUPS + q * RQ
                        mm = transpose(o[:, at:at + RQ], table[0:RQ, q, h * 128:(h + 1) * 128], RQ)
                mm.then_inc(s_tabT, 1)
            for c in range(4):
                mm = transpose(psB[0:1, 0, c * RQ:(c + 1) * RQ], tab_cols[0:RQ, c:c + 1], RQ)
            mm.then_inc(s_tabT, 1)
            pe.wait_ge(s_wts, 48)
            for h in range(2):
                for q in range(2):
                    at = h * GROUPS + q * RQ
                    mm = transpose(psB[:, 1, at:at + RQ], rows_w[0:RQ, q, h * 128:(h + 1) * 128], RQ)
            mm.then_inc(s_tabT, 1)

            pe.wait_ge(s_par, 7 * 16)
            pe.wait_ge(s_tabE, 14)
            for m in range(4):
                if m >= 2:
                    pe.wait_ge(s_wTe, m - 1)
                if m == 3:
                    pe.wait_ge(s_fold, KC + 2 + 2 * KC)
                for ki in range(KC):
                    for ko in range(KC):
                        w = w_raw[:, m, ko, ki * 128:(ki + 1) * 128] if m < 3 else w_fold[:, ko, ki * 128:(ki + 1) * 128]
                        mm = transpose(psB[:, m % 2, ki * C + ko * 128:ki * C + (ko + 1) * 128], w, 128)
                mm.then_inc(s_wTt, 1)
            pe.wait_ge(s_wTe, 4)
            for k in range(KC):
                mm = nc.tensor.matmul(psB[0:P, 0, 0:C], lnb_mat[:, k, :], wT_all[:, 2, k, :], start=(k == 0), stop=(k == KC - 1))
            mm.then_inc(s_bff, 1)
            pe.wait_ge(s_ln1, NT)
            for t in range(NT + 1):
                if t < NT:
                    if t >= 2:
                        pe.wait_ge(s_xTe, t - 1)
                    for k in range(KC):
                        mm = transpose(psA[:, t % 2, k * P:(k + 1) * P], work[:, t, k * 128:(k + 1) * 128], P)
                    mm.then_inc(s_xT, 1)
                if t >= 1:
                    n = t - 1
                    pe.wait_ge(s_xTe, n + 1)
                    if n == 1:
                        pe.wait_ge(s_fold, KC + 2 + 2 * KC + 1)
                    if n >= 2:
                        pe.wait_ge(s_selfe, n - 1)
                    for k in range(KC):
                        mm = nc.tensor.matmul(psB[0:P, (n + 1) % 2, 0:C], hT[:, n, k, :], wT_all[:, 0, k, :],
                                              start=(k == 0), stop=(k == KC - 1))
                    mm.then_inc(s_self, 1)
            pe.wait_ge(s_selfe, NT)
            pe.wait_ge(s_cst, 5)
            windows = pe.alloc_register("tensor_windows")
            pe.reg_mov(windows, 0)
            with pe.Fori(0, BODIES) as i:
                for j in range(HALF):
                    g = i * HALF + j
                    count = pe.value_load(tab[0:1, 1, bass.ds(g, 1)], min_val=1, max_val=SPAN // W)
                    done = pe.snap(windows, min_val=0, max_val=GROUPS * (SPAN // W))
                    with pe.Fori(0, count) as k:
                        for h in range(2):
                            pe.wait_ge(s_g[2 * j + h], i * 16 + 16)
                        pe.wait_ge(s_num, done + k + 1)
                        pe.wait_ge(s_oh, (done + k) * 2 + 2)
                        for c in range(KC + 1):
                            for h in range(2):
                                rows = gath[:, 2 * j + h, c * 128:(c + 1) * 128] if c < KC else ones[:, :]
                                mm = nc.tensor.matmul(psB[:, 0, c * W:(c + 1) * W], rows, onehot[:, h, :],
                                                      start=(h == 0), stop=(h == 1))
                        mm.then_inc(s_win, 1)
                    pe.reg_add(windows, windows, count)
            pe.wait_ge(s_neigh, 2 + KC)
            for t in range(NT):
                if t >= 2:
                    pe.wait_ge(s_gsum, t - 1)
                for k in range(KC):
                    mm = nc.tensor.matmul(psB[0:P, t % 2, 0:C], numT[:, k, t * P:(t + 1) * P], wT_all[:, 1, k, :],
                                          start=(k == 0), stop=(k == KC - 1))
                mm.then_inc(s_np, 1)
            pe.wait_ge(s_gsum, NT)

            def transposes(k, g):
                pe.wait_ge(s_silu, k + 1)
                for n, (a, b) in enumerate(PAIRS):
                    if n == 2:
                        pe.wait_ge(s_hTe, k * 3 + 1)
                    for j in range(a, b):
                        for c in range(KC):
                            mm = transpose(psA[:, n % 2, ((j - a) * KC + c) * P:((j - a) * KC + c + 1) * P],
                                           work[:, g * GT + j, c * 128:(c + 1) * 128], P)
                    mm.then_inc(s_hT, 1)

            def products(k, g):
                for n, (a, b) in enumerate(PAIRS):
                    pe.wait_ge(s_hTe, k * 3 + (n + 1))
                    for j in range(a, b):
                        for c in range(KC):
                            mm = nc.tensor.matmul(psB[0:P, g % 2, j * C:(j + 1) * C], hT[:, g * GT + j, c, :],
                                                  wT_all[:, 3, c, :], start=(c == 0), stop=(c == KC - 1))
                        mm.then_inc(s_z, 1)

            with pe.Fori(0, STEPS) as it:
                for g in range(NG):
                    k = it * NG + g
                    transposes(k, g)
                    if g == 1:
                        pe.wait_ge(s_y, it * NG + NG)
                    if g:
                        if g >= 3:
                            pe.wait_ge(s_y, it * NG + NG + (g - 2))
                        products(k - 1, g - 1)
                pe.wait_ge(s_y, it * NG + NG + 3)
                products(it * NG + NG - 1, NG - 1)


_INS = ['x', 'src', 'dst', 'edge_weight', 'L0_gnn_W_self', 'L0_gnn_W_neigh', 'L0_gnn_bias', 'L0_ffn_ln_w',
        'L0_ffn_ln_b', 'L0_ffn_W', 'L0_ffn_b']


def kernel(**inputs):
    import numpy as _np
    import concourse.bacc as _bacc
    from concourse import mybir as _mybir
    from concourse.bass_utils import run_bass_kernel_spmd as _run

    nc = _bacc.Bacc("TRN2", target_bir_lowering=False, num_devices=1)
    arrays, args = {}, []
    for name in _INS:
        a = _np.ascontiguousarray(inputs[name])
        arrays[f"in_{name}_dram"] = a
        args.append(nc.dram_tensor(f"in_{name}_dram", a.shape, _mybir.dt.from_np(a.dtype), kind="ExternalInput").ap())
    out = nc.dram_tensor("out_0_dram", inputs['x'].shape, _mybir.dt.float32, kind="ExternalOutput").ap()
    gnn_ffn_kernel(nc, *args, out)
    r = _run(nc, [arrays], core_ids=[0])
    return r.results[0]["out_0_dram"]
```

```python
from contextlib import ExitStack

import concourse.bass as bass
from concourse import mybir

F32 = mybir.dt.float32
I32 = mybir.dt.int32
ALU = mybir.AluOpType
ACT = mybir.ActivationFunctionType
AX_X = mybir.AxisListType.X


def gnn_ffn_kernel(nc, x, src, dst, edge_weight, w_self, w_neigh, gnn_bias, ln_w, ln_b, w_ffn, b_ffn, out):
    N, C = x.shape
    E = src.shape[0]
    STEPS = 30
    LN_EPS = 1e-5
    EPS_WSUM = 1e-8
    EPS_NORM = 1e-12
    P = 125
    NT = N // P
    KC = C // 128
    GT = 5
    NG = NT // GT
    W = 64
    W_SHIFT = 6
    EG = 256
    RQ = 98
    GROUPS = 2 * RQ
    LAST = E - (GROUPS - 1) * EG
    SPAN = N + W
    RING = 28
    RG = RING // 2
    SEG = 4
    SEGS = RING // SEG
    BODIES = GROUPS // RG
    assert N == NT * P and NT == NG * GT and C == 256 and 0 < LAST <= EG and E >= EG
    assert NT * KC * P <= RING * C and GROUPS % RG == 0 and RING % SEG == 0 and 1 << W_SHIFT == W

    ln1_dram = nc.dram_tensor("ln1_scratch", [N, C], F32, kind="Internal").ap()

    with ExitStack() as ctx:
        def sb(name, shape, dt=F32):
            return ctx.enter_context(nc.sbuf_tensor(name, shape, dt))

        def sem(name):
            return ctx.enter_context(nc.semaphore(name))

        x_sb = sb("x_sb", [P, NT, C])
        y_sb = sb("y_sb", [P, NT, C])
        work = sb("work", [P, NT, C])
        gath = sb("gath", [128, RING, C])
        hT = gath[:, :, :].rearrange("p r c -> p (r c)")[:, 0:NT * KC * P].rearrange(
            "p (t k n) -> p t k n", t=NT, k=KC)
        lnT = sb("lnT", [128, 2, KC, P])
        numT = sb("numT", [128, KC + 1, SPAN])
        iota_f = sb("iota_f", [128, SPAN])
        small_i = sb("small_i", [128, 2, EG], I32)
        rows_w = sb("rows_w", [128, 2, EG])
        rows_d = sb("rows_d", [128, 2, EG])
        rows_s = sb("rows_s", [128, 2, EG])
        src_i = sb("src_i", [128, 2, EG], I32)
        tab_cols = sb("tab_cols", [128, 4])
        tab_max = sb("tab_max", [128, 2])
        tab_int = sb("tab_int", [128, 2], I32)
        tab = sb("tab", [1, GROUPS, 2], I32)
        dstT = sb("dstT", [128, GROUPS + 1, 2])
        wT = sb("wT", [128, GROUPS + 1, 2])
        srcT = sb("srcT", [128, GROUPS * 2 + RING], I32)
        idx = sb("idx", [128, RING], I32)
        onehot = sb("onehot", [128, 2, 2, W])
        ident = sb("ident", [128, 128])
        ones = sb("ones", [128, 128])
        w_raw = sb("w_raw", [128, 3, KC, C])
        w_fold = sb("w_fold", [128, KC, C])
        wT_all = sb("wT_all", [128, 4, KC, C])
        rowmean = sb("rowmean", [128, KC])
        lnw_bc = sb("lnw_bc", [128, C])
        bias_bc = sb("bias_bc", [P, C])
        bff_bc = sb("bff_bc", [P, C])
        lnb_col = sb("lnb_col", [128, KC])
        lnb_mat = sb("lnb_mat", [128, KC, P])
        st = sb("st", [P, NT, 6])
        mv = sb("mv", [P, NT, 2])
        rstd = sb("rstd", [P, NT])
        ssq = sb("ssq", [P, NT])
        sd = sb("sd", [P, NT])
        mhalf = sb("mhalf", [P, GT])
        quarter = sb("quarter", [P, GT])
        ceps = sb("ceps", [P, GT])
        pl = sb("pl", [P, NG, 6, GT])

        psA = ctx.enter_context(nc.psum_tensor("psA", [128, 2, 512], F32))
        psB = ctx.enter_context(nc.psum_tensor("psB", [128, 2, 1536], F32))

        s_dst = sem("dst_loaded")
        s_src = sem("src_loaded")
        s_wts = sem("edge_weights_loaded")
        s_x = [sem(f"x_loaded_{g}") for g in range(NG)]
        s_par = sem("parameters_loaded")
        s_ident = sem("ident_made")
        s_cst = sem("constants_made")
        s_dve = sem("vector_chain")
        s_act = sem("scalar_chain")
        s_tabT = sem("table_transposed")
        s_tabE = sem("table_evicted")
        s_stat0 = sem("x_stats_ready")
        s_ln1 = sem("ln1_made")
        s_ln1w = sem("ln1_in_dram")
        s_wTt = sem("weights_transposed")
        s_wTe = sem("weights_evicted")
        s_fold = sem("weights_folded")
        s_bff = sem("ffn_bias_product")
        s_xT = sem("ln1_transposed")
        s_xTe = sem("ln1T_evicted")
        s_self = sem("self_product")
        s_selfe = sem("self_evicted")
        s_idx = sem("indices_ready")
        s_g = [sem(f"gathered_{r}") for r in range(RING)]
        s_oh = sem("onehot_ready")
        s_go = sem("gathers_go")
        s_win = sem("window_product")
        s_num = sem("window_added")
        s_pad = sem("padding_made")
        s_xoh = sem("extra_onehot_ready")
        s_xwin = sem("extra_window_product")
        s_xnum = sem("extra_window_added")
        s_neigh = sem("neigh_ready")
        s_np = sem("neigh_product")
        s_gsum = sem("gnn_row_summed")
        s_ss = sem("row_squares_summed")
        s_var = sem("x_variance_ready")
        s_sd = sem("deviation_ready")
        s_rec = sem("x_rstd_ready")
        s_y = sem("rows_ready")
        s_tanh = sem("tanh_ready")
        s_u = sem("u_ready")
        s_silu = sem("silu_ready")
        s_bn = sem("stats_ready")
        s_rstd = sem("rstd_ready")
        s_pool = sem("pool_chain")
        s_hT = sem("h_transposed")
        s_hTe = sem("hT_evicted")
        s_z = sem("ffn_product")
        s_res = sem("result_ready")
        s_out = sem("out_written")

        block = ctx.enter_context(nc.Block())

        x_dram = x.rearrange("(t p) c -> p t c", p=P)
        ln1_out = ln1_dram.rearrange("(t p) c -> p t c", p=P)
        out_dram = out.rearrange("(t p) c -> p t c", p=P)
        PAIRS = [(0, 2), (2, 4), (4, 5)]

        def load_edges(eng, table, tile, s):
            full = table[0:RQ * EG].rearrange("(r k) -> r k", k=EG)
            eng.dma_start(tile[0:RQ, 0, :], full).then_inc(s, 16)
            rest = table[RQ * EG:(GROUPS - 1) * EG].rearrange("(r k) -> r k", k=EG)
            eng.dma_start(tile[0:RQ - 1, 1, :], rest).then_inc(s, 16)
            tail = table[(GROUPS - 1) * EG:E].rearrange("(a k) -> a k", a=1)
            eng.dma_start(tile[RQ - 1:RQ, 1, 0:LAST], tail).then_inc(s, 16)

        def fill_edges(eng, table, tile, s):
            fill = table[E - (EG - LAST):E].rearrange("(a k) -> a k", a=1)
            eng.dma_start(tile[RQ - 1:RQ, 1, LAST:EG], fill).then_inc(s, 16)

        @block.sync
        def _(sp):
            load_edges(sp, dst, small_i, s_dst)
            fill_edges(sp, dst, small_i, s_dst)
            for g in range(NG):
                sp.dma_start(x_sb[:, g * GT:(g + 1) * GT, :], x_dram[:, g * GT:(g + 1) * GT, :]).then_inc(s_x[g], 16)
            for m, w in enumerate((w_self, w_neigh, w_ffn)):
                sp.dma_start(w_raw[:, m, :, :], w.rearrange("(k p) c -> p k c", p=128)).then_inc(s_par, 16)
            sp.dma_start(lnw_bc[:], ln_w.rearrange("(a c) -> a c", a=1).broadcast_to([128, C])).then_inc(s_par, 16)
            sp.dma_start(bias_bc[:], gnn_bias.rearrange("(a c) -> a c", a=1).broadcast_to([P, C])).then_inc(s_par, 16)
            sp.dma_start(bff_bc[:], b_ffn.rearrange("(a c) -> a c", a=1).broadcast_to([P, C])).then_inc(s_par, 16)
            sp.dma_start(lnb_col[:], ln_b.rearrange("(k p) -> p k", p=128), allow_slow_non_contiguous=True).then_inc(s_par, 16)
            for g in range(NG):
                sp.wait_ge(s_ln1, (g + 1) * GT)
                sp.dma_start(ln1_out[:, g * GT:(g + 1) * GT, :], work[:, g * GT:(g + 1) * GT, :]).then_inc(s_ln1w, 16)
            for g in range(NG):
                sp.wait_ge(s_res, g + 1)
                sp.dma_start(out_dram[:, g * GT:(g + 1) * GT, :], y_sb[:, g * GT:(g + 1) * GT, :]).then_inc(s_out, 16)
            sp.wait_ge(s_out, 16 * NG)
            sp.wait_ge(s_ln1w, 16 * NG)

        @block.gpsimd
        def _(pool):
            nc.gpsimd.memset(ident[:], 0.0).then_inc(s_pool, 1)
            pool.wait_ge(s_pool, 1)
            nc.gpsimd.affine_select(out=ident[:], in_=ident[:], compare_op=ALU.not_equal, fill=1.0, base=0,
                                    pattern=[[-1, 128]], channel_multiplier=1).then_inc(s_ident, 1)
            nc.gpsimd.memset(ones[:], 1.0).then_inc(s_cst, 1)
            nc.gpsimd.iota(iota_f[:], pattern=[[1, SPAN]], base=0, channel_multiplier=0,
                           allow_small_or_imprecise_dtypes=True).then_inc(s_cst, 1)
            nc.gpsimd.memset(mhalf[:], -0.5).then_inc(s_cst, 1)
            nc.gpsimd.memset(quarter[:], C / 4.0).then_inc(s_cst, 1)
            nc.gpsimd.memset(ceps[:], C * LN_EPS).then_inc(s_cst, 1)
            nc.gpsimd.memset(numT[:], 0.0).then_inc(s_num, 1)
            pool.wait_ge(s_ln1w, 16 * NG)
            with pool.Fori(0, BODIES) as i:
                for seg in range(SEGS):
                    pool.wait_ge(s_idx, i * SEGS + (seg + 1))
                    pool.sem_inc(s_go, 1)
                    for r in range(seg * SEG, (seg + 1) * SEG):
                        nc.gpsimd.indirect_dma_start(
                            out=gath[:, r, :], out_offset=None, in_=ln1_dram[:, :],
                            in_offset=bass.IndirectOffsetOnAxis(ap=idx[:, r:r + 1], axis=0)).then_inc(s_g[r], 16)

            def rstd_of(k, g):
                sg = st[:, g * GT:(g + 1) * GT, :]
                pool.wait_ge(s_bn, (k + 1) * GT)
                nc.gpsimd.tensor_tensor(pl[:, g, 0, :], sg[:, :, 1], sg[:, :, 4], ALU.subtract).then_inc(s_pool, 1)
                nc.gpsimd.tensor_tensor(pl[:, g, 1, :], sg[:, :, 2], sg[:, :, 5], ALU.add).then_inc(s_pool, 1)
                pool.wait_ge(s_pool, k * 6 + 3)
                nc.gpsimd.tensor_tensor(pl[:, g, 2, :], pl[:, g, 0, :], pl[:, g, 0, :], ALU.mult).then_inc(s_pool, 1)
                pool.wait_ge(s_pool, k * 6 + 4)
                nc.gpsimd.tensor_tensor(pl[:, g, 3, :], pl[:, g, 2, :], quarter[:, :], ALU.mult).then_inc(s_pool, 1)
                pool.wait_ge(s_pool, k * 6 + 5)
                nc.gpsimd.tensor_tensor(pl[:, g, 4, :], pl[:, g, 3, :], pl[:, g, 1, :], ALU.add).then_inc(s_pool, 1)
                pool.wait_ge(s_pool, k * 6 + 6)
                nc.gpsimd.tensor_tensor(pl[:, g, 5, :], pl[:, g, 4, :], ceps[:, :], ALU.add).then_inc(s_pool, 1)
                pool.wait_ge(s_pool, k * 6 + 7)
                nc.gpsimd.tensor_tensor(rstd[:, g * GT:(g + 1) * GT], pl[:, g, 5, :], mhalf[:, :], ALU.pow).then_inc(s_rstd, 1)

            pool.wait_ge(s_cst, 5)
            pool.wait_ge(s_y, NG)
            with pool.Fori(0, STEPS) as it:
                for g in range(NG):
                    rstd_of(it * NG + g, g)

        @block.scalar
        def _(act):
            load_edges(act, src, src_i, s_src)
            fill_edges(act, src, src_i, s_src)
            act.wait_ge(s_dve, 1)
            load_edges(act, edge_weight, rows_w, s_wts)

            for g in range(NG):
                act.wait_ge(s_var, g + 1)
                nc.scalar.activation(sd[:, g * GT:(g + 1) * GT], rstd[:, g * GT:(g + 1) * GT], ACT.Sqrt).then_inc(s_sd, 1)
            for m in range(4):
                act.wait_ge(s_wTt, m + 1)
                nc.scalar.copy(wT_all[:, m, :, :], psB[:, m % 2, 0:KC * C].rearrange("p (k c) -> p k c", k=KC)).then_inc(s_wTe, 1)
            for t in range(NT):
                act.wait_ge(s_xT, t + 1)
                if t >= 2:
                    act.wait_ge(s_self, t - 1)
                nc.scalar.copy(lnT[:, t % 2, :, :], psA[:, t % 2, 0:KC * P].rearrange("p (k n) -> p k n", k=KC)).then_inc(s_xTe, 1)
            for t in range(NT):
                act.wait_ge(s_gsum, t + 1)
                nc.scalar.activation(work[:, t, :], y_sb[:, t, :], ACT.Square, accum_out=ssq[:, t:t + 1]).then_inc(s_ss, 1)
            act.wait_ge(s_ss, NT)
            nc.scalar.activation(sd[:, :], ssq[:, :], ACT.Sqrt).then_inc(s_sd, 1)
            act.wait_ge(s_dve, 4)
            nc.scalar.activation(sd[:, :], rstd[:, :], ACT.Sqrt).then_inc(s_sd, 1)

            def evict(k, g):
                for n, (a, b) in enumerate(PAIRS):
                    act.wait_ge(s_hT, k * 3 + (n + 1))
                    nc.scalar.copy(hT[:, g * GT + a:g * GT + b, :, :],
                                   psA[:, n % 2, 0:(b - a) * KC * P].rearrange("p (j k n) -> p j k n", k=KC, n=P)
                                   ).then_inc(s_hTe, 1)

            act.wait_ge(s_sd, NG + 2)
            with act.Fori(0, STEPS) as it:
                for g in range(NG):
                    k = it * NG + g
                    rows = slice(g * GT, (g + 1) * GT)
                    act.wait_ge(s_y, k + 1)
                    nc.scalar.activation(work[:, rows, :], y_sb[:, rows, :], ACT.Tanh).then_inc(s_tanh, 1)
                    if g:
                        evict(k - 1, g - 1)
                    act.wait_ge(s_u, k + 1)
                    nc.scalar.activation(work[:, rows, :], work[:, rows, :], ACT.Silu).then_inc(s_silu, 1)
                evict(it * NG + (NG - 1), NG - 1)

        @block.vector
        def _(dve):
            nc.vector.memset(rows_w[:], 0.0).then_inc(s_dve, 1)
            nc.vector.memset(srcT[:], 0).then_inc(s_tabE, 1)
            nc.vector.memset(dstT[:, GROUPS, :], 0.0).then_inc(s_pad, 1)
            nc.vector.memset(wT[:, GROUPS, :], 0.0).then_inc(s_pad, 1)
            nc.vector.memset(tab_max[:], 0.0).then_inc(s_xnum, 1)

            dve.wait_ge(s_dst, 64)
            nc.vector.tensor_copy(rows_d[0:RQ, :, :], small_i[0:RQ, :, :]).then_inc(s_tabE, 1)
            dve.wait_ge(s_tabE, 2)
            nc.vector.tensor_reduce(tab_cols[0:RQ, 0:2], rows_d[0:RQ, :, :], AX_X, ALU.min).then_inc(s_tabE, 1)
            nc.vector.tensor_reduce(tab_max[0:RQ, :], rows_d[0:RQ, :, :], AX_X, ALU.max).then_inc(s_tabE, 1)
            dve.wait_ge(s_tabE, 4)
            nc.vector.tensor_tensor(tab_int[0:RQ, :], tab_max[0:RQ, :], tab_cols[0:RQ, 0:2], ALU.subtract).then_inc(s_tabE, 1)
            for q in range(2):
                nc.vector.tensor_scalar(rows_d[0:RQ, q, :], rows_d[0:RQ, q, :], tab_cols[0:RQ, q:q + 1], None,
                                        ALU.subtract).then_inc(s_tabE, 1)
            dve.wait_ge(s_tabE, 7)
            nc.vector.tensor_scalar(small_i[0:RQ, 0, 0:2], tab_int[0:RQ, :], W_SHIFT, None,
                                    ALU.arith_shift_right).then_inc(s_tabE, 1)
            dve.wait_ge(s_tabE, 8)
            nc.vector.tensor_scalar(tab_cols[0:RQ, 2:4], small_i[0:RQ, 0, 0:2], 1.0, None, ALU.add).then_inc(s_tabE, 1)
            dve.wait_ge(s_src, 64)
            nc.vector.tensor_copy(rows_s[0:RQ, :, :], src_i[0:RQ, :, :]).then_inc(s_tabE, 1)
            def x_stats(g):
                tiles = range(g * GT, (g + 1) * GT)
                dve.wait_ge(s_x[g], 16)
                for t in tiles:
                    nc.vector.bn_stats(st[:, t, :], x_sb[:, t, :]).then_inc(s_stat0, 1)
                dve.wait_ge(s_stat0, g * 2 * GT + GT)
                for t in tiles:
                    nc.vector.bn_aggr(mv[:, t, :], st[:, t, :]).then_inc(s_stat0, 1)
                dve.wait_ge(s_stat0, (g + 1) * 2 * GT)
                nc.vector.tensor_scalar(rstd[:, g * GT:(g + 1) * GT], mv[:, g * GT:(g + 1) * GT, 1], LN_EPS, None,
                                        ALU.add).then_inc(s_var, 1)

            def x_scale(g):
                dve.wait_ge(s_sd, g + 1)
                nc.vector.reciprocal(ssq[:, g * GT:(g + 1) * GT], sd[:, g * GT:(g + 1) * GT]).then_inc(s_rec, 1)
                dve.wait_ge(s_rec, g + 1)
                for t in range(g * GT, (g + 1) * GT):
                    nc.vector.tensor_scalar(work[:, t, :], x_sb[:, t, :], mv[:, t, 0:1], ssq[:, t:t + 1],
                                            ALU.subtract, ALU.mult).then_inc(s_ln1, 1)

            x_stats(0)
            per = GROUPS * 2
            dve.wait_ge(s_tabT, 1)
            nc.vector.tensor_copy(srcT[:, 0:per].rearrange("p (g h) -> p h g", h=2),
                                  psA[:, 0, 0:per].rearrange("p (h g) -> p h g", h=2)).then_inc(s_tabE, 1)
            dve.wait_ge(s_tabT, 2)
            nc.vector.tensor_copy(dstT[:, 0:GROUPS, :].rearrange("p g h -> p h g"),
                                  psA[:, 1, 0:per].rearrange("p (h g) -> p h g", h=2)).then_inc(s_tabE, 1)
            dve.wait_ge(s_tabT, 3)
            nc.vector.tensor_copy(tab[:, :, :].rearrange("p g a -> p a g"), psB[0:1, 0, 0:2 * GROUPS].rearrange("p (a g) -> p a g", a=2)).then_inc(s_tabE, 1)
            dve.wait_ge(s_tabT, 4)
            nc.vector.tensor_copy(wT[:, 0:GROUPS, :].rearrange("p g h -> p h g"),
                                  psB[:, 1, 0:per].rearrange("p (h g) -> p h g", h=2)).then_inc(s_tabE, 1)
            dve.wait_ge(s_tabE, 14)
            for seg in range(SEGS):
                a = seg * SEG
                nc.vector.tensor_copy(idx[:, a:a + SEG], srcT[:, a:a + SEG]).then_inc(s_idx, 1)
            for g in range(NG):
                if g + 1 < NG:
                    x_stats(g + 1)
                x_scale(g)

            dve.wait_ge(s_par, 7 * 16)
            for k in range(KC):
                nc.vector.tensor_tensor(w_fold[:, k, :], w_raw[:, 2, k, :], lnw_bc[:, :], ALU.mult).then_inc(s_fold, 1)
            dve.wait_ge(s_fold, KC)
            nc.vector.tensor_reduce(rowmean[:, :], w_fold[:, :, :], AX_X, ALU.add).then_inc(s_fold, 1)
            dve.wait_ge(s_fold, KC + 1)
            nc.vector.tensor_scalar(tab_max[:, :], rowmean[:, :], 1.0 / C, None, ALU.mult).then_inc(s_fold, 1)
            dve.wait_ge(s_fold, KC + 2)
            for k in range(KC):
                nc.vector.tensor_scalar(w_fold[:, k, :], w_fold[:, k, :], tab_max[:, k:k + 1], float(C) ** 0.5,
                                        ALU.subtract, ALU.mult).then_inc(s_fold, 1)
            for k in range(KC):
                nc.vector.tensor_copy(lnb_mat[:, k, :], lnb_col[:, k:k + 1].broadcast_to([128, P])).then_inc(s_fold, 1)
            dve.wait_ge(s_bff, 1)
            nc.vector.tensor_tensor(bff_bc[:, :], bff_bc[:, :], psB[0:P, 0, 0:C], ALU.add).then_inc(s_fold, 1)
            for t in range(NT):
                dve.wait_ge(s_self, t + 1)
                nc.vector.tensor_tensor(y_sb[:, t, :], psB[0:P, (t + 1) % 2, 0:C], bias_bc[:, :], ALU.add).then_inc(s_selfe, 1)

            extra = dve.alloc_register("vector_extra_windows")
            column = dve.alloc_register("window_column")
            entry = [dve.alloc_register(f"vector_entry_{n}") for n in range(2 * RG)]
            dve.reg_mov(extra, 0)

            def make_onehot(o, g, k, s):
                for h in range(2):
                    nc.vector.tensor_scalar(o[:, h, :], iota_f[:, 0:W] if k is None else iota_f[:, bass.ds(k * W, W)],
                                            dstT[:, bass.ds(g, 1), h], wT[:, bass.ds(g, 1), h],
                                            ALU.is_equal, ALU.mult).then_inc(s, 1)

            def add_window(at, slot, s):
                cols = numT[:, :, bass.ds(at, W)]
                nc.vector.tensor_tensor(cols, cols, psB[:, slot, 0:(KC + 1) * W].rearrange("p (c w) -> p c w", w=W),
                                        ALU.add).then_inc(s, 1)

            dve.wait_ge(s_pad, 2)
            dve.wait_ge(s_cst, 5)
            make_onehot(onehot[:, 0, :, :], 0, None, s_oh)
            with dve.Fori(0, BODIES) as i:
                dve.load(entry, tab[0:1, bass.ds(i * RG, RG), :].rearrange("a g b -> a (g b)"))
                for j in range(RG):
                    g = i * RG + j
                    make_onehot(onehot[:, (j + 1) % 2, :, :], g + 1, None, s_oh)
                    dve.wait_ge(s_win, g + 1)
                    dve.wait_ge(s_num, g + 1)
                    dve.wait_ge(s_xnum, dve.snap(extra, min_val=0, max_val=GROUPS * SPAN // W) + 1)
                    add_window(dve.snap(entry[2 * j], min_val=0, max_val=N - 1), j % 2, s_num)
                    count = dve.snap(entry[2 * j + 1], min_val=1, max_val=SPAN // W)
                    with dve.If(count > 1):
                        dve.reg_add(column, entry[2 * j], W)
                        with dve.Fori(1, count) as k:
                            done = dve.snap(extra, min_val=0, max_val=GROUPS * SPAN // W)
                            make_onehot(onehot[:, j % 2, :, :], g, k, s_xoh)
                            dve.wait_ge(s_num, g + 2)
                            dve.wait_ge(s_xnum, done + 1)
                            dve.wait_ge(s_xwin, done + 1)
                            add_window(dve.snap(column, min_val=0, max_val=N - 1), j % 2, s_xnum)
                            dve.reg_add(column, column, W)
                            dve.reg_add(extra, extra, 1)
                    if j % 2:
                        a = (j // 2) * SEG
                        nc.vector.tensor_copy(idx[:, a:a + SEG],
                                              srcT[:, bass.ds((i + 1) * RING + a, SEG)]).then_inc(s_idx, 1)

            dve.wait_ge(s_idx, SEGS * (BODIES + 1))
            nc.vector.tensor_scalar(numT[:, KC, 0:N], numT[:, KC, 0:N], EPS_WSUM, None, ALU.max).then_inc(s_neigh, 1)
            dve.wait_ge(s_neigh, 1)
            nc.vector.reciprocal(numT[:, KC, 0:N], numT[:, KC, 0:N]).then_inc(s_neigh, 1)
            dve.wait_ge(s_neigh, 2)
            for k in range(KC):
                nc.vector.tensor_tensor(numT[:, k, 0:N], numT[:, k, 0:N], numT[:, KC, 0:N], ALU.mult).then_inc(s_neigh, 1)
            for t in range(NT):
                dve.wait_ge(s_np, t + 1)
                nc.vector.tensor_tensor(y_sb[:, t, :], psB[0:P, t % 2, 0:C], y_sb[:, t, :], ALU.add).then_inc(s_gsum, 1)
            dve.wait_ge(s_sd, NG + 1)
            nc.vector.tensor_scalar(rstd[:, :], sd[:, :], EPS_NORM, None, ALU.max).then_inc(s_dve, 1)
            dve.wait_ge(s_dve, 2)
            nc.vector.reciprocal(ssq[:, :], rstd[:, :]).then_inc(s_dve, 1)
            dve.wait_ge(s_dve, 3)
            for t in range(NT):
                nc.vector.scalar_tensor_tensor(out=x_sb[:, t, :], in0=y_sb[:, t, :], scalar=ssq[:, t:t + 1],
                                               in1=x_sb[:, t, :], op0=ALU.mult, op1=ALU.add).then_inc(s_neigh, 1)
            for t in range(NT):
                dve.wait_ge(s_neigh, 2 + KC + t + 1)
                nc.vector.bn_stats(st[:, t, :], x_sb[:, t, :]).then_inc(s_neigh, 1)
            dve.wait_ge(s_neigh, 2 + KC + 2 * NT)
            for t in range(NT):
                nc.vector.bn_aggr(mv[:, t, :], st[:, t, :]).then_inc(s_neigh, 1)
            dve.wait_ge(s_neigh, 2 + KC + 3 * NT)
            nc.vector.tensor_scalar(rstd[:, :], mv[:, :, 1], LN_EPS, None, ALU.add).then_inc(s_dve, 1)
            dve.wait_ge(s_sd, NG + 2)
            nc.vector.reciprocal(ssq[:, :], sd[:, :]).then_inc(s_dve, 1)
            dve.wait_ge(s_dve, 5)
            for t in range(NT):
                ins = nc.vector.tensor_scalar(y_sb[:, t, :], x_sb[:, t, :], mv[:, t, 0:1], ssq[:, t:t + 1],
                                              ALU.subtract, ALU.mult)
                if t % GT == GT - 1:
                    ins.then_inc(s_y, 1)

            def rows_of(g):
                return slice(g * GT, (g + 1) * GT)

            def make_u(k, g):
                dve.wait_ge(s_tanh, k + 1)
                nc.vector.scalar_tensor_tensor(out=work[:, rows_of(g), :], in0=work[:, rows_of(g), :], scalar=0.01,
                                               in1=y_sb[:, rows_of(g), :], op0=ALU.mult, op1=ALU.add).then_inc(s_u, 1)

            def stats(k, g):
                dve.wait_ge(s_silu, k + 1)
                for t in range(g * GT, (g + 1) * GT):
                    nc.vector.bn_stats(st[:, t, :], work[:, t, :]).then_inc(s_bn, 1)

            def next_rows(k, g):
                dve.wait_ge(s_rstd, k + 1)
                for j in range(GT):
                    if j % 2 == 0:
                        dve.wait_ge(s_z, k * GT + min(j + 2, GT))
                    ins = nc.vector.scalar_tensor_tensor(
                        out=y_sb[:, g * GT + j, :], in0=psB[0:P, g % 2, j * C:(j + 1) * C],
                        scalar=rstd[:, g * GT + j:g * GT + j + 1], in1=bff_bc[:, :], op0=ALU.mult, op1=ALU.add)
                ins.then_inc(s_y, 1)

            def step(it, first):
                for g in range(NG):
                    k = it * NG + g
                    make_u(k, g)
                    if g < 2:
                        if not first:
                            next_rows(k - 2, g + NG - 2)
                    if g:
                        stats(k - 1, g - 1)
                    if g >= 2:
                        next_rows(k - 2, g - 2)
                stats(it * NG + NG - 1, NG - 1)

            step(0, True)
            with dve.Fori(1, STEPS) as it:
                step(it, False)
            for g in (NG - 2, NG - 1):
                next_rows((STEPS - 1) * NG + g, g)
            for g in range(NG):
                dve.wait_ge(s_y, (STEPS + 1) * NG - (NG - 1 - g))
                nc.vector.tensor_tensor(y_sb[:, rows_of(g), :], y_sb[:, rows_of(g), :], x_sb[:, rows_of(g), :],
                                        ALU.add).then_inc(s_res, 1)

        @block.tensor
        def _(pe):
            def transpose(o, i, n):
                return nc.tensor.transpose(o, i, ident[0:n, 0:n])

            pe.wait_ge(s_ident, 1)
            pe.wait_ge(s_tabE, 10)
            for table, o, s in ((rows_s, psA[:, 0, :], None), (rows_d, psA[:, 1, :], None)):
                for h in range(2):
                    for q in range(2):
                        at = h * GROUPS + q * RQ
                        mm = transpose(o[:, at:at + RQ], table[0:RQ, q, h * 128:(h + 1) * 128], RQ)
                mm.then_inc(s_tabT, 1)
            for c in range(4):
                mm = transpose(psB[0:1, 0, c * RQ:(c + 1) * RQ], tab_cols[0:RQ, c:c + 1], RQ)
            mm.then_inc(s_tabT, 1)
            pe.wait_ge(s_wts, 48)
            for h in range(2):
                for q in range(2):
                    at = h * GROUPS + q * RQ
                    mm = transpose(psB[:, 1, at:at + RQ], rows_w[0:RQ, q, h * 128:(h + 1) * 128], RQ)
            mm.then_inc(s_tabT, 1)

            pe.wait_ge(s_par, 7 * 16)
            pe.wait_ge(s_tabE, 14)
            for m in range(4):
                if m >= 2:
                    pe.wait_ge(s_wTe, m - 1)
                if m == 3:
                    pe.wait_ge(s_fold, KC + 2 + 2 * KC)
                for ki in range(KC):
                    for ko in range(KC):
                        w = w_raw[:, m, ko, ki * 128:(ki + 1) * 128] if m < 3 else w_fold[:, ko, ki * 128:(ki + 1) * 128]
                        mm = transpose(psB[:, m % 2, ki * C + ko * 128:ki * C + (ko + 1) * 128], w, 128)
                mm.then_inc(s_wTt, 1)
            pe.wait_ge(s_wTe, 4)
            for k in range(KC):
                mm = nc.tensor.matmul(psB[0:P, 0, 0:C], lnb_mat[:, k, :], wT_all[:, 2, k, :], start=(k == 0), stop=(k == KC - 1))
            mm.then_inc(s_bff, 1)
            pe.wait_ge(s_ln1, NT)
            for t in range(NT + 1):
                if t < NT:
                    if t >= 2:
                        pe.wait_ge(s_xTe, t - 1)
                    for k in range(KC):
                        mm = transpose(psA[:, t % 2, k * P:(k + 1) * P], work[:, t, k * 128:(k + 1) * 128], P)
                    mm.then_inc(s_xT, 1)
                if t >= 1:
                    n = t - 1
                    pe.wait_ge(s_xTe, n + 1)
                    if n == 1:
                        pe.wait_ge(s_fold, KC + 2 + 2 * KC + 1)
                    if n >= 2:
                        pe.wait_ge(s_selfe, n - 1)
                    for k in range(KC):
                        mm = nc.tensor.matmul(psB[0:P, (n + 1) % 2, 0:C], lnT[:, n % 2, k, :], wT_all[:, 0, k, :],
                                              start=(k == 0), stop=(k == KC - 1))
                    mm.then_inc(s_self, 1)
            pe.wait_ge(s_selfe, NT)
            pe.wait_ge(s_cst, 5)
            extra = pe.alloc_register("tensor_extra_windows")
            entry = [pe.alloc_register(f"tensor_entry_{n}") for n in range(2 * RG)]
            pe.reg_mov(extra, 0)

            def window(j, s):
                for c in range(KC + 1):
                    for h in range(2):
                        rows = gath[:, 2 * j + h, c * 128:(c + 1) * 128] if c < KC else ones[:, :]
                        mm = nc.tensor.matmul(psB[:, j % 2, c * W:(c + 1) * W], rows, onehot[:, j % 2, h, :],
                                              start=(h == 0), stop=(h == 1))
                mm.then_inc(s, 1)

            pe.wait_ge(s_num, 1)
            with pe.Fori(0, BODIES) as i:
                pe.load(entry, tab[0:1, bass.ds(i * RG, RG), :].rearrange("a g b -> a (g b)"))
                for j in range(RG):
                    g = i * RG + j
                    for h in range(2):
                        pe.wait_ge(s_g[2 * j + h], i * 16 + 16)
                    pe.wait_ge(s_oh, g * 2 + 2)
                    window(j, s_win)
                    count = pe.snap(entry[2 * j + 1], min_val=1, max_val=SPAN // W)
                    with pe.If(count > 1):
                        with pe.Fori(1, count) as k:
                            pe.wait_ge(s_xoh, pe.snap(extra, min_val=0, max_val=GROUPS * SPAN // W) * 2 + 2)
                            window(j, s_xwin)
                            pe.reg_add(extra, extra, 1)
            pe.wait_ge(s_neigh, 2 + KC)
            for t in range(NT):
                if t >= 2:
                    pe.wait_ge(s_gsum, t - 1)
                for k in range(KC):
                    mm = nc.tensor.matmul(psB[0:P, t % 2, 0:C], numT[:, k, t * P:(t + 1) * P], wT_all[:, 1, k, :],
                                          start=(k == 0), stop=(k == KC - 1))
                mm.then_inc(s_np, 1)
            pe.wait_ge(s_gsum, NT)

            def transposes(k, g):
                pe.wait_ge(s_silu, k + 1)
                for n, (a, b) in enumerate(PAIRS):
                    if n == 2:
                        pe.wait_ge(s_hTe, k * 3 + 1)
                    for j in range(a, b):
                        for c in range(KC):
                            mm = transpose(psA[:, n % 2, ((j - a) * KC + c) * P:((j - a) * KC + c + 1) * P],
                                           work[:, g * GT + j, c * 128:(c + 1) * 128], P)
                    mm.then_inc(s_hT, 1)

            def products(k, g):
                for n, (a, b) in enumerate(PAIRS):
                    pe.wait_ge(s_hTe, k * 3 + (n + 1))
                    for j in range(a, b):
                        for c in range(KC):
                            mm = nc.tensor.matmul(psB[0:P, g % 2, j * C:(j + 1) * C], hT[:, g * GT + j, c, :],
                                                  wT_all[:, 3, c, :], start=(c == 0), stop=(c == KC - 1))
                        mm.then_inc(s_z, 1)

            with pe.Fori(0, STEPS) as it:
                for g in range(NG):
                    k = it * NG + g
                    transposes(k, g)
                    if g == 1:
                        pe.wait_ge(s_y, it * NG + NG)
                    if g:
                        if g >= 3:
                            pe.wait_ge(s_y, it * NG + NG + (g - 2))
                        products(k - 1, g - 1)
                pe.wait_ge(s_y, it * NG + NG + 3)
                products(it * NG + NG - 1, NG - 1)


_INS = ['x', 'src', 'dst', 'edge_weight', 'L0_gnn_W_self', 'L0_gnn_W_neigh', 'L0_gnn_bias', 'L0_ffn_ln_w',
        'L0_ffn_ln_b', 'L0_ffn_W', 'L0_ffn_b']


def kernel(**inputs):
    import numpy as _np
    import concourse.bacc as _bacc
    from concourse import mybir as _mybir
    from concourse.bass_utils import run_bass_kernel_spmd as _run

    nc = _bacc.Bacc("TRN2", target_bir_lowering=False, num_devices=1)
    arrays, args = {}, []
    for name in _INS:
        a = _np.ascontiguousarray(inputs[name])
        arrays[f"in_{name}_dram"] = a
        args.append(nc.dram_tensor(f"in_{name}_dram", a.shape, _mybir.dt.from_np(a.dtype), kind="ExternalInput").ap())
    out = nc.dram_tensor("out_0_dram", inputs['x'].shape, _mybir.dt.float32, kind="ExternalOutput").ap()
    gnn_ffn_kernel(nc, *args, out)
    r = _run(nc, [arrays], core_ids=[0])
    return r.results[0]["out_0_dram"]
```

```python
from contextlib import ExitStack

import concourse.bass as bass
from concourse import mybir

F32 = mybir.dt.float32
F16 = mybir.dt.float16
I32 = mybir.dt.int32
ALU = mybir.AluOpType
ACT = mybir.ActivationFunctionType
AX_X = mybir.AxisListType.X


def gnn_ffn_kernel(nc, x, src, dst, edge_weight, w_self, w_neigh, gnn_bias, ln_w, ln_b, w_ffn, b_ffn, out):
    N, C = x.shape
    E = src.shape[0]
    STEPS = 30
    LN_EPS = 1e-5
    EPS_WSUM = 1e-8
    EPS_NORM = 1e-12
    Y_SCALE = 100.0
    P = 125
    NT = N // P
    PT = 128
    KC = C // 128
    GT = 5
    NG = NT // GT
    W = 64
    W_SHIFT = 6
    EG = 256
    RQ = 98
    GROUPS = 2 * RQ
    LAST = E - (GROUPS - 1) * EG
    SPAN = NT * PT
    SHIFT = 0.25
    RING = 28
    RG = RING // 2
    SEG = 4
    SEGS = RING // SEG
    BODIES = GROUPS // RG
    assert GT == 5 and SPAN >= N + W and N == NT * P and NT == NG * GT and C == 256 and 0 < LAST <= EG and E >= EG
    assert NT * KC * P <= RING * C and GROUPS % RG == 0 and RING % SEG == 0 and 1 << W_SHIFT == W

    ln1_dram = nc.dram_tensor("ln1_scratch", [N, C], F32, kind="Internal").ap()

    with ExitStack() as ctx:
        def sb(name, shape, dt=F32):
            return ctx.enter_context(nc.sbuf_tensor(name, shape, dt))

        def sem(name):
            return ctx.enter_context(nc.semaphore(name))

        x_sb = sb("x_sb", [P, NT, C])
        y_sb = sb("y_sb", [P, NT, C])
        work = sb("work", [P, NT, C])
        gath = sb("gath", [128, RING, C])
        hT = gath[:, :, :].rearrange("p r c -> p (r c)").bitcast(F16)[:, 0:NT * KC * 2 * PT].rearrange(
            "p (t k s n) -> p t k s n", t=NT, k=KC, s=2)[:, :, :, :, 0:P]
        row_slot = sb("row_slot", [P, 2, C])
        lnT = sb("lnT", [128, 2, KC, P])
        numT = sb("numT", [128, KC, SPAN])
        h16 = numT[0:P, :, :].rearrange("p a c -> p (a c)").bitcast(F16)[:, 0:NT * 2 * C].rearrange(
            "p (s t c) -> p s t c", t=NT, s=2)
        iota_f = sb("iota_f", [128, SPAN])
        small_i = sb("small_i", [128, 2, EG], I32)
        rows_w = sb("rows_w", [128, 2, EG])
        rows_d = sb("rows_d", [128, 2, EG])
        rows_s = sb("rows_s", [128, 2, EG])
        src_i = sb("src_i", [128, 2, EG], I32)
        tab_cols = sb("tab_cols", [128, 4])
        tab_max = sb("tab_max", [128, 2])
        tab_int = sb("tab_int", [128, 2], I32)
        tab = sb("tab", [1, GROUPS, 2], I32)
        dstT = sb("dstT", [128, GROUPS + 1, 2])
        wT = sb("wT", [128, GROUPS + 1, 2])
        srcT = sb("srcT", [128, GROUPS * 2 + RING], I32)
        idx = sb("idx", [128, RING], I32)
        onehot = sb("onehot", [128, 2, 2, W])
        touch = sb("touch", [128, 1])
        touched = sb("touched", [128, 1])
        ident = sb("ident", [128, 128])
        ident16 = sb("ident16", [128, 128], F16)
        neighT = sb("neighT", [128, KC, C + 1])
        w_raw = sb("w_raw", [128, 3, KC, C])
        w_fold = sb("w_fold", [128, KC, C])
        wT_all = sb("wT_all", [128, 4, KC, C])
        w16 = sb("w16", [128, 2, KC, C], F16)
        rowsum = sb("rowsum", [128, 3, KC])
        rowmean = sb("rowmean", [128, 3, KC])
        lnw_bc = sb("lnw_bc", [128, C])
        bias_bc = sb("bias_bc", [P, C])
        bff_bc = sb("bff_bc", [P, C])
        lnb_col = sb("lnb_col", [128, KC])
        lnb_mat = sb("lnb_mat", [128, KC, P])
        st = sb("st", [P, NT, 6])
        mv = sb("mv", [P, NT, 2])
        rstd = sb("rstd", [P, NT])
        ssq = sb("ssq", [P, NT])
        sd = sb("sd", [P, NT])
        var = sb("var", [P, NT])
        shift = sb("shift", [P, NT])
        norm = sb("norm", [P, NT])
        wsum = sb("wsum", [P, NT])
        mhalf = sb("mhalf", [P, GT])
        var_step = sb("var_step", [P, NG, 4, GT])

        ZB = 5
        psA = ctx.enter_context(nc.psum_tensor("psA", [128, 3, 512], F32))
        psB = ctx.enter_context(nc.psum_tensor("psB", [128, ZB, 512], F32))

        s_dst = sem("dst_loaded")
        s_src = sem("src_loaded")
        s_wts = sem("edge_weights_loaded")
        s_x = [sem(f"x_loaded_{g}") for g in range(NG)]
        s_par = sem("parameters_loaded")
        s_ident = sem("ident_made")
        s_cst = sem("constants_made")
        s_touch = sem("touch_made")
        s_dve = sem("vector_chain")
        s_idxT = sem("sources_transposed")
        s_idxE = sem("sources_evicted")
        s_tabT = sem("table_transposed")
        s_tabE = sem("table_evicted")
        s_stat0 = sem("x_stats_ready")
        s_ln1 = sem("ln1_made")
        s_ln1v = sem("ln1_last_group_made")
        s_ln1w = sem("ln1_in_dram")
        s_wTt = sem("weights_transposed")
        s_wTe = sem("weights_evicted")
        s_fold = sem("weights_folded")
        s_bff = sem("ffn_bias_product")
        s_row = sem("row_slot_filled")
        s_xT = sem("ln1_transposed")
        s_xTe = sem("ln1T_evicted")
        s_self = sem("self_product")
        s_selfe = sem("self_summed")
        s_idx = sem("indices_ready")
        s_g = [sem(f"gathered_{r}") for r in range(RING)]
        s_oh = sem("onehot_ready")
        s_go = sem("gathers_go")
        s_win = sem("window_product")
        s_num = sem("window_added")
        s_pad = sem("padding_made")
        s_xoh = sem("extra_onehot_ready")
        s_xwin = sem("extra_window_product")
        s_xnum = sem("extra_window_added")
        s_rw = sem("weight_sums_inverted")
        s_norm = sem("norms_ready")
        s_sum = sem("residual_and_stats")
        s_rstd1 = sem("first_rstd_ready")
        s_shift = sem("first_shift_ready")
        s_np = sem("neigh_product")
        s_gsum = sem("gnn_row_summed")
        s_ss = sem("row_squares_summed")
        s_var = sem("x_variance_ready")
        s_sd = sem("deviation_ready")
        s_rec = sem("x_rstd_ready")
        s_first = sem("first_rows_ready")
        s_y = sem("rows_ready")
        s_tanh = sem("tanh_ready")
        s_u = [sem(f"u_ready_{g}") for g in range(NG)]
        s_silu = sem("silu_ready")
        s_w16 = sem("split_weights_ready")
        s_hi = [sem(f"high_part_ready_{g}") for g in range(NG)]
        s_lo = sem("low_part_ready")
        s_bn = sem("stats_ready")
        s_rstd = sem("rstd_ready")
        s_dev = sem("variance_chain")
        s_vare = sem("variance_ready")
        s_pool = sem("pool_chain")
        s_hT = sem("h_transposed")
        s_hTe = sem("hT_evicted")
        s_z = sem("ffn_product")
        s_res = sem("result_ready")
        s_out = sem("out_written")

        block = ctx.enter_context(nc.Block())

        x_dram = x.rearrange("(t p) c -> p t c", p=P)
        ln1_out = ln1_dram.rearrange("(t p) c -> p t c", p=P)
        out_dram = out.rearrange("(t p) c -> p t c", p=P)
        psT = psA[:, :, :].rearrange("p b c -> p (b c)").bitcast(F16).rearrange("p (m n) -> p m n", n=PT)
        PAIRS = [(0, 2), (2, 4), (4, 5)]
        NP = len(PAIRS)
        HI_ON_ACT = (0, 2, 4)
        U_ON_POOL = (2, 4)
        K_END = STEPS * NG
        FOLDED = KC + 3 + 4 * KC
        LEAD = 2
        LAG = 4

        def rows_of(g):
            return slice(g * GT, (g + 1) * GT)

        def z_bank(g, n):
            return (g * NP + n) % ZB

        def before(k, g, d, start, end):
            if end and g - d >= 0:
                return None
            if start and g - d < 0:
                return None
            return k - d, (g - d) % NG

        def ffn_slots(eng, slot, layer_step=None):
            if layer_step:
                for i in range(LEAD):
                    layer_step(i)
            for g in range(NG):
                if layer_step:
                    layer_step(g + LEAD)
                slot(g, g, True, False)
            with eng.Fori(1, STEPS) as it:
                for g in range(NG):
                    slot(it * NG + g, g, False, False)
            for g in range(LAG):
                slot(K_END + g, g, False, True)

        RUNS = [(0, NT // 2, 2), (NT // 2, NT // 2 + 1, 1), (NT // 2 + 1, BODIES, 0)]
        TRANSPOSE_AT, PRODUCT_AT, SUM_AT = (2, 9), (4, 11), (5, 12)
        assert NT % 2 == 1 and BODIES > NT // 2 + 1

        def load_edges(eng, table, tile, s):
            full = table[0:RQ * EG].rearrange("(r k) -> r k", k=EG)
            eng.dma_start(tile[0:RQ, 0, :], full).then_inc(s, 16)
            rest = table[RQ * EG:(GROUPS - 1) * EG].rearrange("(r k) -> r k", k=EG)
            eng.dma_start(tile[0:RQ - 1, 1, :], rest).then_inc(s, 16)
            tail = table[(GROUPS - 1) * EG:E].rearrange("(a k) -> a k", a=1)
            eng.dma_start(tile[RQ - 1:RQ, 1, 0:LAST], tail).then_inc(s, 16)

        def fill_edges(eng, table, tile, s):
            fill = table[E - (EG - LAST):E].rearrange("(a k) -> a k", a=1)
            eng.dma_start(tile[RQ - 1:RQ, 1, LAST:EG], fill).then_inc(s, 16)

        @block.sync
        def _(sp):
            for g in range(NG):
                sp.dma_start(x_sb[:, g * GT:(g + 1) * GT, :], x_dram[:, g * GT:(g + 1) * GT, :]).then_inc(s_x[g], 16)
            load_edges(sp, dst, small_i, s_dst)
            fill_edges(sp, dst, small_i, s_dst)
            for m, w in enumerate((w_self, w_neigh, w_ffn)):
                sp.dma_start(w_raw[:, m, :, :], w.rearrange("(k p) c -> p k c", p=128)).then_inc(s_par, 16)
            sp.dma_start(lnw_bc[:], ln_w.rearrange("(a c) -> a c", a=1).broadcast_to([128, C])).then_inc(s_par, 16)
            sp.dma_start(bias_bc[:], gnn_bias.rearrange("(a c) -> a c", a=1).broadcast_to([P, C])).then_inc(s_par, 16)
            sp.dma_start(bff_bc[:], b_ffn.rearrange("(a c) -> a c", a=1).broadcast_to([P, C])).then_inc(s_par, 16)
            sp.dma_start(lnb_col[:], ln_b.rearrange("(k p) -> p k", p=128), allow_slow_non_contiguous=True).then_inc(s_par, 16)
            for g in range(NG):
                if g < NG - 1:
                    sp.wait_ge(s_ln1, (g + 1) * GT)
                else:
                    sp.wait_ge(s_ln1v, GT)
                sp.dma_start(ln1_out[:, g * GT:(g + 1) * GT, :], work[:, g * GT:(g + 1) * GT, :]).then_inc(s_ln1w, 16)
            for g in range(NG):
                sp.wait_ge(s_res, g + 1)
                sp.dma_start(out_dram[:, g * GT:(g + 1) * GT, :], y_sb[:, g * GT:(g + 1) * GT, :]).then_inc(s_out, 16)
            sp.wait_ge(s_out, 16 * NG)
            sp.wait_ge(s_ln1w, 16 * NG)

        @block.gpsimd
        def _(pool):
            nc.gpsimd.memset(ident[:], 0.0).then_inc(s_pool, 1)
            pool.wait_ge(s_pool, 1)
            nc.gpsimd.affine_select(out=ident[:], in_=ident[:], compare_op=ALU.not_equal, fill=1.0, base=0,
                                    pattern=[[-1, 128]], channel_multiplier=1).then_inc(s_ident, 1)
            nc.gpsimd.memset(neighT[:, :, C:C + 1], 1.0 / (SHIFT * C)).then_inc(s_cst, 1)
            nc.gpsimd.iota(iota_f[:], pattern=[[1, SPAN]], base=0, channel_multiplier=0,
                           allow_small_or_imprecise_dtypes=True).then_inc(s_cst, 1)
            nc.gpsimd.memset(mhalf[:], -0.5).then_inc(s_cst, 1)
            nc.gpsimd.memset(numT[:], 0.0).then_inc(s_num, 1)
            pool.wait_ge(s_ln1w, 16 * NG)
            with pool.Fori(0, BODIES) as i:
                for seg in range(SEGS):
                    pool.wait_ge(s_idx, i * SEGS + (seg + 1))
                    pool.sem_inc(s_go, 1)
                    for r in range(seg * SEG, (seg + 1) * SEG):
                        nc.gpsimd.indirect_dma_start(
                            out=gath[:, r, :], out_offset=None, in_=ln1_dram[:, :],
                            in_offset=bass.IndirectOffsetOnAxis(ap=idx[:, r:r + 1], axis=0)).then_inc(s_g[r], 16)

            def layer_step(g):
                if g < NG:
                    pool.wait_ge(s_ss, (g + 1) * GT)
                    nc.gpsimd.tensor_scalar(ssq[:, rows_of(g)], ssq[:, rows_of(g)], EPS_NORM ** 2, None, ALU.max).then_inc(s_pool, 1)
                    pool.wait_ge(s_pool, g + 2)
                    nc.gpsimd.tensor_tensor(norm[:, rows_of(g)], ssq[:, rows_of(g)], mhalf[:, :], ALU.pow).then_inc(s_norm, 1)
                if 1 <= g <= NG:
                    n = g - 1
                    pool.wait_ge(s_var, NG + n + 1)
                    nc.gpsimd.tensor_tensor(rstd[:, rows_of(n)], var[:, rows_of(n)], mhalf[:, :], ALU.pow).then_inc(s_rstd1, 1)

            def low_part(k, g):
                pool.wait_ge(s_hi[g], k + (NG - g))
                nc.gpsimd.tensor_tensor(h16[:, 1, rows_of(g), :], work[:, rows_of(g), :], h16[:, 0, rows_of(g), :],
                                        ALU.subtract).then_inc(s_lo, 1)

            def sum_u(k, g):
                if g in U_ON_POOL:
                    pool.wait_ge(s_tanh, k + 1)
                    nc.gpsimd.tensor_tensor(work[:, rows_of(g), :], work[:, rows_of(g), :], y_sb[:, rows_of(g), :],
                                            ALU.add).then_inc(s_u[g], NG)

            def rstd_of(k, g):
                pool.wait_ge(s_vare, k + 1)
                nc.gpsimd.tensor_tensor(rstd[:, rows_of(g)], var_step[:, g, 3, :], mhalf[:, :], ALU.pow).then_inc(s_rstd, 1)

            def slot(k, g, start, end):
                if not end:
                    sum_u(k, g)
                if b := before(k, g, 3, start, end):
                    rstd_of(*b)
                if b := before(k, g, 1, start, end):
                    low_part(*b)

            pool.wait_ge(s_cst, 3)
            ffn_slots(pool, slot, layer_step)

        @block.scalar
        def _(act):
            load_edges(act, src, src_i, s_src)
            fill_edges(act, src, src_i, s_src)
            act.wait_ge(s_dve, 1)
            load_edges(act, edge_weight, rows_w, s_wts)

            def deviation(g):
                act.wait_ge(s_var, g + 1)
                nc.scalar.activation(sd[:, rows_of(g)], var[:, rows_of(g)], ACT.Sqrt).then_inc(s_sd, 1)

            deviation(0)
            for g in range(NG - 1):
                deviation(g + 1)
                act.wait_ge(s_rec, 3 * g + 3)
                for t in range(g * GT, (g + 1) * GT):
                    nc.scalar.activation(work[:, t, :], x_sb[:, t, :], ACT.Identity, bias=shift[:, t:t + 1],
                                         scale=rstd[:, t:t + 1]).then_inc(s_ln1, 1)
            for m in range(4):
                act.wait_ge(s_wTt, m + 1)
                nc.scalar.copy(neighT[:, :, 0:C] if m == 1 else wT_all[:, m, :, :], psB[:, m % 2, 0:KC * C].rearrange("p (k c) -> p k c", k=KC)).then_inc(s_wTe, 1)
            act.wait_ge(s_touch, 1)
            nc.scalar.activation(touched[:], touch[:], ACT.Silu)
            for first, end, tiles in RUNS[0:2]:
                act.wait_ge(s_ln1v, GT)
                with act.Fori(first, end) as i:
                    for u in range(tiles):
                        nc.scalar.copy(row_slot[:, u, :], work[:, bass.ds(i * 2 + u, 1), :].rearrange("p a c -> p (a c)")).then_inc(s_row, 1)
                        act.wait_ge(s_xT, i * 2 + (u + 1))
                        nc.scalar.copy(lnT[:, u, :, :], psA[:, u, 0:KC * P].rearrange("p (k n) -> p k n", k=KC)).then_inc(s_xTe, 1)

            def squares(g):
                for t in range(g * GT, (g + 1) * GT):
                    act.wait_ge(s_gsum, t + 1)
                    nc.scalar.activation(work[:, t, :], y_sb[:, t, :], ACT.Square, accum_out=ssq[:, t:t + 1]).then_inc(s_ss, 1)

            def first_rows(g):
                act.wait_ge(s_shift, g + 1)
                for t in range(g * GT, (g + 1) * GT):
                    ins = nc.scalar.activation(y_sb[:, t, :], x_sb[:, t, :], ACT.Identity, bias=shift[:, t:t + 1],
                                               scale=rstd[:, t:t + 1])
                ins.then_inc(s_first, 1)

            def layer_step(g):
                if g < NG:
                    squares(g)
                if g >= LEAD:
                    first_rows(g - LEAD)

            def evict(k, g):
                act.wait_ge(s_hT, k + 1)
                nc.scalar.copy(hT[:, rows_of(g), :, :, :].rearrange("p j k s n -> p (j k s) n"),
                               psT[:, 0:GT * KC * 2, 0:P]).then_inc(s_hTe, 1)

            def tanh_rows(k, g, start):
                if start:
                    act.wait_ge(s_first, g + 1)
                else:
                    act.wait_ge(s_y, (k - NG) * NP + (NP + ZB))
                nc.scalar.activation(work[:, rows_of(g), :], y_sb[:, rows_of(g), :], ACT.Tanh, scale=1.0 / Y_SCALE).then_inc(s_tanh, 1)

            def silu_rows(k, g):
                act.wait_ge(s_u[g], k + (NG - g))
                nc.scalar.activation(work[:, rows_of(g), :], work[:, rows_of(g), :], ACT.Silu, scale=1.0 / Y_SCALE).then_inc(s_silu, 1)

            def high_part(k, g):
                if g in HI_ON_ACT:
                    act.wait_ge(s_silu, k + 1)
                    act.wait_ge(s_np, NT)
                    nc.scalar.copy(h16[:, 0, rows_of(g), :], work[:, rows_of(g), :]).then_inc(s_hi[g], NG)

            def slot(k, g, start, end):
                if not end:
                    tanh_rows(k, g, start)
                if b := before(k, g, 3, start, end):
                    evict(*b)
                if b := before(k, g, 1, start, end):
                    silu_rows(*b)
                if b := before(k, g, 1, start, end):
                    high_part(*b)

            ffn_slots(act, slot, layer_step)

        @block.vector
        def _(dve):
            nc.vector.memset(touch[:], 0.0).then_inc(s_touch, 1)
            nc.vector.memset(rows_w[:], 0.0).then_inc(s_dve, 1)
            nc.vector.memset(srcT[:], 0).then_inc(s_idxE, 1)
            nc.vector.memset(dstT[:, GROUPS, :], 0.0).then_inc(s_pad, 1)
            nc.vector.memset(wT[:, GROUPS, :], 0.0).then_inc(s_pad, 1)
            nc.vector.memset(tab_max[:], 0.0).then_inc(s_xnum, 1)

            def group_tables():
                dve.wait_ge(s_dst, 64)
                nc.vector.tensor_copy(rows_d[0:RQ, :, :], small_i[0:RQ, :, :]).then_inc(s_tabE, 1)
                dve.wait_ge(s_tabE, 1)
                nc.vector.tensor_reduce(tab_cols[0:RQ, 0:2], rows_d[0:RQ, :, :], AX_X, ALU.min).then_inc(s_tabE, 1)
                nc.vector.tensor_reduce(tab_max[0:RQ, :], rows_d[0:RQ, :, :], AX_X, ALU.max).then_inc(s_tabE, 1)
                dve.wait_ge(s_tabE, 3)
                nc.vector.tensor_tensor(tab_int[0:RQ, :], tab_max[0:RQ, :], tab_cols[0:RQ, 0:2], ALU.subtract).then_inc(s_tabE, 1)
                for q in range(2):
                    nc.vector.tensor_scalar(rows_d[0:RQ, q, :], rows_d[0:RQ, q, :], tab_cols[0:RQ, q:q + 1], None,
                                            ALU.subtract).then_inc(s_tabE, 1)
                dve.wait_ge(s_tabE, 6)
                nc.vector.tensor_scalar(small_i[0:RQ, 0, 0:2], tab_int[0:RQ, :], W_SHIFT, None,
                                        ALU.arith_shift_right).then_inc(s_tabE, 1)
                dve.wait_ge(s_tabE, 7)
                nc.vector.tensor_scalar(tab_cols[0:RQ, 2:4], small_i[0:RQ, 0, 0:2], 1.0, None, ALU.add).then_inc(s_tabE, 1)

            def x_stats(g):
                tiles = range(g * GT, (g + 1) * GT)
                dve.wait_ge(s_x[g], 16)
                for t in tiles:
                    nc.vector.bn_stats(st[:, t, :], x_sb[:, t, :]).then_inc(s_stat0, 1)
                dve.wait_ge(s_stat0, g * 2 * GT + GT)
                for t in tiles:
                    nc.vector.bn_aggr(mv[:, t, :], st[:, t, :]).then_inc(s_stat0, 1)
                dve.wait_ge(s_stat0, (g + 1) * 2 * GT)
                nc.vector.tensor_scalar(var[:, rows_of(g)], mv[:, rows_of(g), 1], LN_EPS, None, ALU.add).then_inc(s_var, 1)

            def x_factors(g):
                rows = rows_of(g)
                dve.wait_ge(s_sd, g + 1)
                nc.vector.reciprocal(rstd[:, rows], sd[:, rows]).then_inc(s_rec, 1)
                dve.wait_ge(s_rec, 3 * g + 1)
                nc.vector.tensor_tensor(sd[:, rows], mv[:, rows, 0], rstd[:, rows], ALU.mult).then_inc(s_rec, 1)
                dve.wait_ge(s_rec, 3 * g + 2)
                nc.vector.tensor_scalar(shift[:, rows], sd[:, rows], -1.0, SHIFT, ALU.mult, ALU.add).then_inc(s_rec, 1)

            per = GROUPS * 2
            x_stats(0)
            for g in range(NG):
                if g + 1 < NG:
                    x_stats(g + 1)
                x_factors(g)
                if g == 0:
                    dve.wait_ge(s_src, 64)
                    nc.vector.tensor_copy(rows_s[0:RQ, :, :], src_i[0:RQ, :, :]).then_inc(s_idxE, 1)
                if g == 1:
                    dve.wait_ge(s_idxT, 1)
                    nc.vector.tensor_copy(srcT[:, 0:per].rearrange("p (g h) -> p h g", h=2),
                                          psA[:, 0, 0:per].rearrange("p (h g) -> p h g", h=2)).then_inc(s_idxE, 1)
                if g == 2:
                    dve.wait_ge(s_idxE, 3)
                    for a in range(0, RING, SEG):
                        nc.vector.tensor_copy(idx[:, a:a + SEG], srcT[:, a:a + SEG]).then_inc(s_idx, 1)
            dve.wait_ge(s_rec, 3 * NG)
            for t in range(NT - GT, NT):
                nc.vector.tensor_scalar(work[:, t, :], x_sb[:, t, :], rstd[:, t:t + 1], shift[:, t:t + 1],
                                        ALU.mult, ALU.add).then_inc(s_ln1v, 1)
            group_tables()
            dve.wait_ge(s_tabT, 1)
            nc.vector.tensor_copy(dstT[:, 0:GROUPS, :].rearrange("p g h -> p h g"),
                                  psA[:, 1, 0:per].rearrange("p (h g) -> p h g", h=2)).then_inc(s_tabE, 1)
            dve.wait_ge(s_tabT, 2)
            nc.vector.tensor_copy(tab[:, :, :].rearrange("p g a -> p a g"), psB[0:1, 0, 0:2 * GROUPS].rearrange("p (a g) -> p a g", a=2)).then_inc(s_tabE, 1)
            dve.wait_ge(s_tabT, 3)
            nc.vector.tensor_copy(wT[:, 0:GROUPS, :].rearrange("p g h -> p h g"),
                                  psB[:, 1, 0:per].rearrange("p (h g) -> p h g", h=2)).then_inc(s_tabE, 1)
            dve.wait_ge(s_tabE, 11)

            dve.wait_ge(s_par, 7 * 16)
            for k in range(KC):
                nc.vector.tensor_tensor(w_fold[:, k, :], w_raw[:, 2, k, :], lnw_bc[:, :], ALU.mult).then_inc(s_fold, 1)
            nc.vector.tensor_reduce(rowsum[:, 0:2, :], w_raw[:, 0:2, :, :], AX_X, ALU.add).then_inc(s_fold, 1)
            dve.wait_ge(s_fold, KC + 1)
            nc.vector.tensor_reduce(rowsum[:, 2, :], w_fold[:, :, :], AX_X, ALU.add).then_inc(s_fold, 1)
            dve.wait_ge(s_fold, KC + 2)
            nc.vector.tensor_scalar(rowmean[:, :, :], rowsum[:, :, :], 1.0 / C, None, ALU.mult).then_inc(s_fold, 1)
            dve.wait_ge(s_fold, KC + 3)
            for m in range(2):
                for k in range(KC):
                    nc.vector.tensor_scalar(w_raw[:, m, k, :], w_raw[:, m, k, :], rowmean[:, m, k:k + 1], None,
                                            ALU.subtract).then_inc(s_fold, 1)
            for k in range(KC):
                nc.vector.tensor_scalar(w_fold[:, k, :], w_fold[:, k, :], rowmean[:, 2, k:k + 1], Y_SCALE * float(C) ** 0.5,
                                        ALU.subtract, ALU.mult).then_inc(s_fold, 1)
            for k in range(KC):
                nc.vector.tensor_copy(lnb_mat[:, k, :], lnb_col[:, k:k + 1].broadcast_to([128, P])).then_inc(s_fold, 1)
            dve.wait_ge(s_wTe, 4)
            nc.vector.tensor_copy(w16[:, 0, :, :], wT_all[:, 3, :, :]).then_inc(s_w16, 1)
            dve.wait_ge(s_w16, 1)
            nc.vector.tensor_tensor(w16[:, 1, :, :], wT_all[:, 3, :, :], w16[:, 0, :, :], ALU.subtract).then_inc(s_w16, 1)
            nc.vector.tensor_copy(ident16[:, :], ident[:, :]).then_inc(s_w16, 1)
            dve.wait_ge(s_bff, 1)
            nc.vector.tensor_tensor(bff_bc[:, :], bff_bc[:, :], psB[0:P, 0, 0:C], ALU.add).then_inc(s_fold, 1)
            dve.wait_ge(s_fold, FOLDED + 1)
            nc.vector.tensor_scalar(bff_bc[:, :], bff_bc[:, :], Y_SCALE, None, ALU.mult).then_inc(s_fold, 1)
            dve.sem_inc(s_selfe, 2)

            extra = dve.alloc_register("vector_extra_windows")
            column = dve.alloc_register("window_column")
            entry = [dve.alloc_register(f"vector_entry_{n}") for n in range(2 * RG)]
            dve.reg_mov(extra, 0)

            def make_onehot(o, g, k, s):
                for h in range(2):
                    nc.vector.tensor_scalar(o[:, h, :], iota_f[:, 0:W] if k is None else iota_f[:, bass.ds(k * W, W)],
                                            dstT[:, bass.ds(g, 1), h], wT[:, bass.ds(g, 1), h],
                                            ALU.is_equal, ALU.mult).then_inc(s, 1)

            def add_window(at, slot, s):
                cols = numT[:, :, bass.ds(at, W)]
                nc.vector.tensor_tensor(cols, cols, psB[:, slot, 0:KC * W].rearrange("p (c w) -> p c w", w=W),
                                        ALU.add).then_inc(s, 1)

            def self_sum(t, u):
                dve.wait_ge(s_self, t + 1)
                nc.vector.tensor_tensor(y_sb[:, bass.ds(t, 1), :].rearrange("p a c -> p (a c)"), psB[0:P, 2 + u, 0:C],
                                        bias_bc[:, :], ALU.add).then_inc(s_selfe, 1)

            dve.wait_ge(s_pad, 2)
            dve.wait_ge(s_cst, 3)
            make_onehot(onehot[:, 0, :, :], 0, None, s_oh)
            for first, end, tiles in RUNS:
                with dve.Fori(first, end) as i:
                    dve.load(entry, tab[0:1, bass.ds(i * RG, RG), :].rearrange("a g b -> a (g b)"))
                    for j in range(RG):
                        g = i * RG + j
                        make_onehot(onehot[:, (j + 1) % 2, :, :], g + 1, None, s_oh)
                        dve.wait_ge(s_win, g + 1)
                        dve.wait_ge(s_num, g + 1)
                        dve.wait_ge(s_xnum, dve.snap(extra, min_val=0, max_val=GROUPS * SPAN // W) + 1)
                        add_window(dve.snap(entry[2 * j], min_val=0, max_val=N - 1), j % 2, s_num)
                        count = dve.snap(entry[2 * j + 1], min_val=1, max_val=SPAN // W)
                        with dve.If(count > 1):
                            dve.reg_add(column, entry[2 * j], W)
                            with dve.Fori(1, count) as k:
                                done = dve.snap(extra, min_val=0, max_val=GROUPS * SPAN // W)
                                make_onehot(onehot[:, j % 2, :, :], g, k, s_xoh)
                                dve.wait_ge(s_num, g + 2)
                                dve.wait_ge(s_xnum, done + 1)
                                dve.wait_ge(s_xwin, done + 1)
                                add_window(dve.snap(column, min_val=0, max_val=N - 1), j % 2, s_xnum)
                                dve.reg_add(column, column, W)
                                dve.reg_add(extra, extra, 1)
                        if j % 2:
                            a = (j // 2) * SEG
                            nc.vector.tensor_copy(idx[:, a:a + SEG],
                                                  srcT[:, bass.ds((i + 1) * RING + a, SEG)]).then_inc(s_idx, 1)
                        if j in SUM_AT[0:tiles]:
                            self_sum(i * 2 + SUM_AT.index(j), SUM_AT.index(j))

            def weight_sums(g):
                rows = rows_of(g)
                dve.wait_ge(s_np, (g + 1) * GT)
                nc.vector.tensor_scalar(wsum[:, rows], psB[0:P, :, C], EPS_WSUM, None, ALU.max).then_inc(s_rw, 1)
                dve.wait_ge(s_rw, 2 * g + 1)
                nc.vector.reciprocal(wsum[:, rows], wsum[:, rows]).then_inc(s_rw, 1)
                dve.wait_ge(s_rw, 2 * g + 2)

            def layer_sum(g):
                for t in range(g * GT, (g + 1) * GT):
                    nc.vector.scalar_tensor_tensor(out=y_sb[:, t, :], in0=psB[0:P, t % ZB, 0:C], scalar=wsum[:, t:t + 1],
                                                   in1=y_sb[:, t, :], op0=ALU.mult, op1=ALU.add).then_inc(s_gsum, 1)
                if g == NG - 1:
                    dve.sem_inc(s_y, ZB)

            def residual(g):
                dve.wait_ge(s_norm, g + 1)
                for t in range(g * GT, (g + 1) * GT):
                    nc.vector.scalar_tensor_tensor(out=x_sb[:, t, :], in0=y_sb[:, t, :], scalar=norm[:, t:t + 1],
                                                   in1=x_sb[:, t, :], op0=ALU.mult, op1=ALU.add).then_inc(s_sum, 1)
                for t in range(g * GT, (g + 1) * GT):
                    dve.wait_ge(s_sum, 3 * g * GT + t % GT + 1)
                    nc.vector.bn_stats(st[:, t, :], x_sb[:, t, :]).then_inc(s_sum, 1)
                for t in range(g * GT, (g + 1) * GT):
                    dve.wait_ge(s_sum, (3 * g + 1) * GT + t % GT + 1)
                    nc.vector.bn_aggr(mv[:, t, :], st[:, t, :]).then_inc(s_sum, 1)
                dve.wait_ge(s_sum, 3 * (g + 1) * GT)
                nc.vector.tensor_scalar(var[:, rows_of(g)], mv[:, rows_of(g), 1], LN_EPS, 1.0 / Y_SCALE ** 2,
                                        ALU.add, ALU.mult).then_inc(s_var, 1)

            def first_shift(g):
                dve.wait_ge(s_rstd1, g + 1)
                nc.vector.scalar_tensor_tensor(out=shift[:, rows_of(g)], in0=mv[:, rows_of(g), 0], scalar=-1.0,
                                               in1=rstd[:, rows_of(g)], op0=ALU.mult, op1=ALU.mult).then_inc(s_shift, 1)

            dve.wait_ge(s_selfe, NT + 2)

            def layer_step(g):
                if g < NG:
                    weight_sums(g)
                    layer_sum(g)
                if g >= LEAD:
                    first_shift(g - LEAD)
                if 1 <= g <= NG:
                    residual(g - 1)

            def sum_u(k, g):
                if g not in U_ON_POOL:
                    dve.wait_ge(s_tanh, k + 1)
                    nc.vector.tensor_tensor(work[:, rows_of(g), :], work[:, rows_of(g), :], y_sb[:, rows_of(g), :],
                                            ALU.add).then_inc(s_u[g], NG)

            def high_part(k, g):
                if g in HI_ON_ACT:
                    return
                dve.wait_ge(s_silu, k + 1)
                dve.wait_ge(s_np, NT)
                nc.vector.tensor_copy(h16[:, 0, rows_of(g), :], work[:, rows_of(g), :]).then_inc(s_hi[g], NG)

            def stats(k, g):
                dve.wait_ge(s_silu, k + 1)
                for t in range(g * GT, (g + 1) * GT):
                    nc.vector.bn_stats(st[:, t, :], work[:, t, :]).then_inc(s_bn, 1)

            def differences(k, g):
                sg = st[:, rows_of(g), :]
                dve.wait_ge(s_bn, k * GT + GT)
                nc.vector.tensor_tensor(var_step[:, g, 0, :], sg[:, :, 1], sg[:, :, 4], ALU.subtract).then_inc(s_dev, 1)
                nc.vector.scalar_tensor_tensor(out=var_step[:, g, 1, :], in0=sg[:, :, 2], scalar=C * LN_EPS, in1=sg[:, :, 5],
                                               op0=ALU.add, op1=ALU.add).then_inc(s_dev, 1)

            def square(k, g):
                dve.wait_ge(s_dev, k * 3 + 1)
                nc.vector.scalar_tensor_tensor(out=var_step[:, g, 2, :], in0=var_step[:, g, 0, :], scalar=C / 4.0, in1=var_step[:, g, 0, :],
                                               op0=ALU.mult, op1=ALU.mult).then_inc(s_dev, 1)

            def variance(k, g):
                dve.wait_ge(s_dev, k * 3 + 3)
                nc.vector.tensor_tensor(var_step[:, g, 3, :], var_step[:, g, 2, :], var_step[:, g, 1, :], ALU.add).then_inc(s_vare, 1)

            def next_rows(k, g, n):
                a, b = PAIRS[n]
                dve.wait_ge(s_z, k * NP + (n + 1))
                for j in range(a, b):
                    ins = nc.vector.scalar_tensor_tensor(
                        out=y_sb[:, g * GT + j, :], in0=psB[0:P, z_bank(g, n), (j - a) * C:(j - a + 1) * C],
                        scalar=rstd[:, g * GT + j:g * GT + j + 1], in1=bff_bc[:, :], op0=ALU.mult, op1=ALU.add)
                ins.then_inc(s_y, 1)

            def result(g):
                dve.wait_ge(s_y, (K_END - NG + g + 1) * NP + ZB)
                nc.vector.scalar_tensor_tensor(out=y_sb[:, rows_of(g), :], in0=y_sb[:, rows_of(g), :], scalar=1.0 / Y_SCALE,
                                               in1=x_sb[:, rows_of(g), :], op0=ALU.mult, op1=ALU.add).then_inc(s_res, 1)

            def slot(k, g, start, end):
                if end:
                    result(g)
                b2, b3 = before(k, g, 3, start, end), before(k, g, LAG, start, end)
                if b2:
                    differences(*b2)
                if b3:
                    dve.wait_ge(s_rstd, b3[0] + 1)
                    next_rows(*b3, 0)
                if b2:
                    square(*b2)
                if b3:
                    next_rows(*b3, 1)
                if b2:
                    variance(*b2)
                if b3:
                    next_rows(*b3, 2)
                if b := before(k, g, 2, start, end):
                    stats(*b)
                if not end:
                    sum_u(k, g)
                if b := before(k, g, 1, start, end):
                    high_part(*b)

            ffn_slots(dve, slot, layer_step)
            result(NG - 1)

        @block.tensor
        def _(pe):
            def transpose(o, i, n):
                return nc.tensor.transpose(o, i, ident[0:n, 0:n])

            pe.wait_ge(s_ident, 1)
            def transpose_table(o, table):
                for h in range(2):
                    for q in range(2):
                        at = h * GROUPS + q * RQ
                        mm = transpose(o[:, at:at + RQ], table[0:RQ, q, h * 128:(h + 1) * 128], RQ)
                return mm

            pe.wait_ge(s_idxE, 2)
            transpose_table(psA[:, 0, :], rows_s).then_inc(s_idxT, 1)
            pe.wait_ge(s_tabE, 8)
            transpose_table(psA[:, 1, :], rows_d).then_inc(s_tabT, 1)
            for c in range(4):
                mm = transpose(psB[0:1, 0, c * RQ:(c + 1) * RQ], tab_cols[0:RQ, c:c + 1], RQ)
            mm.then_inc(s_tabT, 1)
            pe.wait_ge(s_wts, 48)
            transpose_table(psB[:, 1, :], rows_w).then_inc(s_tabT, 1)

            pe.wait_ge(s_par, 7 * 16)
            pe.wait_ge(s_tabE, 11)
            pe.wait_ge(s_fold, FOLDED)
            for m in range(4):
                if m >= 2:
                    pe.wait_ge(s_wTe, m - 1)
                for ki in range(KC):
                    for ko in range(KC):
                        w = w_raw[:, m, ko, ki * 128:(ki + 1) * 128] if m < 3 else w_fold[:, ko, ki * 128:(ki + 1) * 128]
                        mm = transpose(psB[:, m % 2, ki * C + ko * 128:ki * C + (ko + 1) * 128], w, 128)
                mm.then_inc(s_wTt, 1)
            pe.wait_ge(s_wTe, 4)
            for k in range(KC):
                mm = nc.tensor.matmul(psB[0:P, 0, 0:C], lnb_mat[:, k, :], wT_all[:, 2, k, :], start=(k == 0), stop=(k == KC - 1))
            mm.then_inc(s_bff, 1)
            pe.wait_ge(s_fold, FOLDED + 1)
            pe.wait_ge(s_cst, 3)
            extra = pe.alloc_register("tensor_extra_windows")
            entry = [pe.alloc_register(f"tensor_entry_{n}") for n in range(2 * RG)]
            pe.reg_mov(extra, 0)

            def window(j, s):
                for c in range(KC):
                    for h in range(2):
                        rows = gath[:, 2 * j + h, c * 128:(c + 1) * 128]
                        mm = nc.tensor.matmul(psB[:, j % 2, c * W:(c + 1) * W], rows, onehot[:, j % 2, h, :],
                                              start=(h == 0), stop=(h == 1))
                mm.then_inc(s, 1)

            def self_transposes(t, u):
                pe.wait_ge(s_row, t + 1)
                for k in range(KC):
                    mm = transpose(psA[:, u, k * P:(k + 1) * P], row_slot[:, u, k * 128:(k + 1) * 128], P)
                mm.then_inc(s_xT, 1)

            def self_product(t, u):
                pe.wait_ge(s_xTe, t + 1)
                pe.wait_ge(s_selfe, t + 1)
                for k in range(KC):
                    mm = nc.tensor.matmul(psB[0:P, 2 + u, 0:C], lnT[:, u, k, :], wT_all[:, 0, k, :],
                                          start=(k == 0), stop=(k == KC - 1))
                mm.then_inc(s_self, 1)

            pe.wait_ge(s_num, 1)
            for first, end, tiles in RUNS:
                with pe.Fori(first, end) as i:
                    pe.load(entry, tab[0:1, bass.ds(i * RG, RG), :].rearrange("a g b -> a (g b)"))
                    for j in range(RG):
                        g = i * RG + j
                        for h in range(2):
                            pe.wait_ge(s_g[2 * j + h], i * 16 + 16)
                        pe.wait_ge(s_oh, g * 2 + 2)
                        window(j, s_win)
                        count = pe.snap(entry[2 * j + 1], min_val=1, max_val=SPAN // W)
                        with pe.If(count > 1):
                            with pe.Fori(1, count) as k:
                                pe.wait_ge(s_xoh, pe.snap(extra, min_val=0, max_val=GROUPS * SPAN // W) * 2 + 2)
                                window(j, s_xwin)
                                pe.reg_add(extra, extra, 1)
                        if j in TRANSPOSE_AT[0:tiles]:
                            self_transposes(i * 2 + TRANSPOSE_AT.index(j), TRANSPOSE_AT.index(j))
                        if j in PRODUCT_AT[0:tiles]:
                            self_product(i * 2 + PRODUCT_AT.index(j), PRODUCT_AT.index(j))

            pe.wait_ge(s_num, GROUPS + 1)
            pe.wait_ge(s_xnum, pe.snap(extra, min_val=0, max_val=GROUPS * SPAN // W) + 1)
            for t in range(NT):
                if t >= ZB:
                    pe.wait_ge(s_gsum, t - ZB + 1)
                for k in range(KC):
                    mm = nc.tensor.matmul(psB[0:P, t % ZB, 0:C + 1], numT[:, k, t * P:(t + 1) * P], neighT[:, k, :],
                                          start=(k == 0), stop=(k == KC - 1))
                mm.then_inc(s_np, 1)
            pe.wait_ge(s_gsum, NT)

            def transposes(k, g):
                pe.wait_ge(s_lo, k + 1)
                for j in range(GT):
                    for c in range(KC):
                        for part in range(2):
                            mm = nc.tensor.transpose(psT[:, (j * KC + c) * 2 + part, 0:P],
                                                     h16[:, part, g * GT + j, c * 128:(c + 1) * 128],
                                                     ident16[0:P, 0:P])
                mm.then_inc(s_hT, 1)

            def products(k, g):
                pe.wait_ge(s_hTe, k + 1)
                for n, (a, b) in enumerate(PAIRS):
                    pe.wait_ge(s_y, k * NP + (n + 1))
                    for j in range(a, b):
                        terms = [(c, hp, wp) for c in range(KC) for hp, wp in ((0, 0), (0, 1), (1, 0))]
                        for c, hp, wp in terms:
                            mm = nc.tensor.matmul(psB[0:P, z_bank(g, n), (j - a) * C:(j - a + 1) * C],
                                                  hT[:, g * GT + j, c, hp, :], w16[:, wp, c, :],
                                                  start=((c, hp, wp) == terms[0]), stop=((c, hp, wp) == terms[-1]))
                    mm.then_inc(s_z, 1)

            def slot(k, g, start, end):
                if b := before(k, g, 4, start, end):
                    products(*b)
                if b := before(k, g, 2, start, end):
                    if c := before(k, g, 3, start, end):
                        pe.wait_ge(s_hTe, c[0] + 1)
                    transposes(*b)

            pe.wait_ge(s_w16, 3)
            ffn_slots(pe, slot)


_INS = ['x', 'src', 'dst', 'edge_weight', 'L0_gnn_W_self', 'L0_gnn_W_neigh', 'L0_gnn_bias', 'L0_ffn_ln_w',
        'L0_ffn_ln_b', 'L0_ffn_W', 'L0_ffn_b']


def kernel(**inputs):
    import numpy as _np
    import concourse.bacc as _bacc
    from concourse import mybir as _mybir
    from concourse.bass_utils import run_bass_kernel_spmd as _run

    nc = _bacc.Bacc("TRN2", target_bir_lowering=False, num_devices=1)
    arrays, args = {}, []
    for name in _INS:
        a = _np.ascontiguousarray(inputs[name])
        arrays[f"in_{name}_dram"] = a
        args.append(nc.dram_tensor(f"in_{name}_dram", a.shape, _mybir.dt.from_np(a.dtype), kind="ExternalInput").ap())
    out = nc.dram_tensor("out_0_dram", inputs['x'].shape, _mybir.dt.float32, kind="ExternalOutput").ap()
    gnn_ffn_kernel(nc, *args, out)
    r = _run(nc, [arrays], core_ids=[0])
    return r.results[0]["out_0_dram"]
```
